# Optimizing a Trainium2 kernel written in Bass

```python
import numpy as np
import jax
import jax.numpy as jnp

def _softmax(x, axis=-1):
    return jax.nn.softmax(x, axis=axis)

def _gelu(x):
    return jax.nn.gelu(x, approximate=True)

def _silu(x):
    return jax.nn.silu(x)

def _sigmoid(x):
    return jax.nn.sigmoid(x)

def _layernorm(x, axis=-1, eps=1e-05):
    m = jnp.mean(x, axis=axis, keepdims=True)
    v = jnp.var(x, axis=axis, keepdims=True)
    return (x - m) / jnp.sqrt(v + eps)

def _scatter_add(tgt, idx, src, axis=0):
    return tgt.at[idx].add(src)

def _segment_sum(src, seg, n):
    return jax.ops.segment_sum(src, seg, n)
kernel_name = 'mk_xattn_ffn_d1_seqx_r8_bc0f2d'

def setup_inputs(seed: int=0):
    np.random.seed(seed)
    _w = jnp.asarray

    def _rec_inputs():
        import jax
        import jax.numpy as jnp
        _rk = jax.random.key(seed)
        x = 0.000341 + 1 * jax.random.normal(jax.random.fold_in(_rk, 1), (16, 128, 256), jnp.float32)
        _lenS = 128 - jax.random.randint(jax.random.fold_in(_rk, 7), (16,), 0, max(1, 128 // 4) + 1, jnp.int32)
        _lenS2 = 128 - jax.random.randint(jax.random.fold_in(_rk, 8), (16,), 0, max(1, 128 // 4) + 1, jnp.int32)
        _ctx_2048P = jax.random.normal(jax.random.fold_in(_rk, 11), (16, 16, 256), jnp.float32)
        _ctx_2048c = jax.random.dirichlet(jax.random.fold_in(_rk, 511), 0.3 * jnp.ones((16,), jnp.float32), (16, 128))
        _ctx_2048t = jnp.einsum('bsk,bkd->bsd', _ctx_2048c, _ctx_2048P)
        _ctx_2048t = _ctx_2048t * jax.lax.rsqrt(jnp.mean(jnp.square(_ctx_2048t)) + 1e-12) * 0.953939
        ctx_2048 = -1.47943e-05 + 1.00017 * (_ctx_2048t + 0.3 * jax.random.normal(jax.random.fold_in(_rk, 611), (16, 128, 256), jnp.float32))
        return (x, ctx_2048)
    x, ctx_2048 = _rec_inputs()

    def _L0_xattn_setup():
        import jax, jax.numpy as jnp
        import numpy as np

        def _wkv(time_decay, time_first, k, v):
            w = -jnp.exp(time_decay)
            u = time_first
            B, T, C = k.shape
            aa = jnp.zeros((B, C), dtype=k.dtype)
            bb = jnp.zeros((B, C), dtype=k.dtype)
            pp = jnp.full((B, C), -1e+38, dtype=k.dtype)

            def step(carry, kv_t):
                aa, bb, pp = carry
                kt, vt = kv_t
                ww = u + kt
                q = jnp.maximum(pp, ww)
                e1 = jnp.exp(pp - q)
                e2 = jnp.exp(ww - q)
                y_t = (e1 * aa + e2 * vt) / (e1 * bb + e2)
                ww2 = pp + w
                q2 = jnp.maximum(ww2, kt)
                e1b = jnp.exp(ww2 - q2)
                e2b = jnp.exp(kt - q2)
                new_carry = (e1b * aa + e2b * vt, e1b * bb + e2b, q2)
                return (new_carry, y_t)
            ks = jnp.transpose(k, (1, 0, 2))
            vs = jnp.transpose(v, (1, 0, 2))
            _, ys = jax.lax.scan(step, (aa, bb, pp), (ks, vs))
            return jnp.transpose(ys, (1, 0, 2))
        key = jax.random.key(seed)
        k1, k2, k3, k4 = jax.random.split(key, 4)
        B, T, C = (8, 128, 256)
        return {'batch_size': B, 'seq_len': T, 'embedding_dim': C, 'time_decay': jax.random.normal(k1, (C,), dtype=jnp.float32), 'time_first': jax.random.normal(k2, (C,), dtype=jnp.float32), 'k': jax.random.normal(k3, (B, T, C), dtype=jnp.float32), 'v': jax.random.normal(k4, (B, T, C), dtype=jnp.float32)}
    _L0_xattn_all = _L0_xattn_setup()
    _L0_xattn_in = {k: v for k, v in _L0_xattn_all.items() if k in ('time_decay', 'time_first')}
    del _L0_xattn_all

    def _L0_ffn_setup():
        import jax, jax.numpy as jnp
        import numpy as np
        HIDDEN = 256
        INTER = 704
        B, S = (2, 256)

        def _ternary(key, shape):
            return jax.random.randint(key, shape, -1, 2).astype(jnp.float32)
        key = jax.random.key(seed)
        ks = jax.random.split(key, 7)
        x = jax.random.normal(ks[0], (B, S, HIDDEN), dtype=jnp.float32)
        gate_w = _ternary(ks[1], (INTER, HIDDEN))
        up_w = _ternary(ks[2], (INTER, HIDDEN))
        down_w = _ternary(ks[3], (HIDDEN, INTER))
        gate_s = jax.random.uniform(ks[4], (INTER,), minval=0.01, maxval=0.1, dtype=jnp.float32)
        up_s = jax.random.uniform(ks[5], (INTER,), minval=0.01, maxval=0.1, dtype=jnp.float32)
        down_s = jax.random.uniform(ks[6], (HIDDEN,), minval=0.01, maxval=0.1, dtype=jnp.float32)
        return {'x': x, 'gate_w': gate_w, 'up_w': up_w, 'down_w': down_w, 'gate_s': gate_s, 'up_s': up_s, 'down_s': down_s}
    _L0_ffn_all = _L0_ffn_setup()
    _L0_ffn_in = {k: v for k, v in _L0_ffn_all.items() if k in ('gate_w', 'up_w', 'down_w', 'gate_s', 'up_s', 'down_s')}
    del _L0_ffn_all
    return {'x': x, 'ctx_2048': ctx_2048, 'L0_xattn_time_decay': _L0_xattn_in['time_decay'], 'L0_xattn_time_first': _L0_xattn_in['time_first'], 'L0_ffn_gate_w': _L0_ffn_in['gate_w'], 'L0_ffn_up_w': _L0_ffn_in['up_w'], 'L0_ffn_down_w': _L0_ffn_in['down_w'], 'L0_ffn_gate_s': _L0_ffn_in['gate_s'], 'L0_ffn_up_s': _L0_ffn_in['up_s'], 'L0_ffn_down_s': _L0_ffn_in['down_s']}

def reference(x, ctx_2048, L0_xattn_time_decay, L0_xattn_time_first, L0_ffn_gate_w, L0_ffn_up_w, L0_ffn_down_w, L0_ffn_gate_s, L0_ffn_up_s, L0_ffn_down_s):
    import jax
    import jax.numpy as jnp

    def _L0_xattn_ref(batch_size, seq_len, embedding_dim, time_decay, time_first, k, v):
        import jax, jax.numpy as jnp
        import numpy as np

        def _wkv(time_decay, time_first, k, v):
            w = -jnp.exp(time_decay)
            u = time_first
            B, T, C = k.shape
            aa = jnp.zeros((B, C), dtype=k.dtype)
            bb = jnp.zeros((B, C), dtype=k.dtype)
            pp = jnp.full((B, C), -1e+38, dtype=k.dtype)

            def step(carry, kv_t):
                aa, bb, pp = carry
                kt, vt = kv_t
                ww = u + kt
                q = jnp.maximum(pp, ww)
                e1 = jnp.exp(pp - q)
                e2 = jnp.exp(ww - q)
                y_t = (e1 * aa + e2 * vt) / (e1 * bb + e2)
                ww2 = pp + w
                q2 = jnp.maximum(ww2, kt)
                e1b = jnp.exp(ww2 - q2)
                e2b = jnp.exp(kt - q2)
                new_carry = (e1b * aa + e2b * vt, e1b * bb + e2b, q2)
                return (new_carry, y_t)
            ks = jnp.transpose(k, (1, 0, 2))
            vs = jnp.transpose(v, (1, 0, 2))
            _, ys = jax.lax.scan(step, (aa, bb, pp), (ks, vs))
            return jnp.transpose(ys, (1, 0, 2))
        assert seq_len <= 128
        return _wkv(time_decay, time_first, k, v)

    def _L0_ffn_ref(x, gate_w, up_w, down_w, gate_s, up_s, down_s):
        import jax, jax.numpy as jnp
        import numpy as np
        HIDDEN = 256
        INTER = 704
        B, S = (2, 256)

        def _ternary(key, shape):
            return jax.random.randint(key, shape, -1, 2).astype(jnp.float32)
        b, s, h = x.shape
        xf = x.reshape(b * s, h)
        g = jnp.einsum('th,ih->ti', xf, gate_w) * gate_s
        u = jnp.einsum('th,ih->ti', xf, up_w) * up_s
        hdn = jax.nn.silu(g) * u
        out = jnp.einsum('ti,hi->th', hdn, down_w) * down_s
        return out.reshape(b, s, -1)
    x = x + _L0_xattn_ref(16, 128, 256, L0_xattn_time_decay, L0_xattn_time_first, _layernorm(x, axis=-1), ctx_2048)
    x = x + _L0_ffn_ref(_layernorm(x, axis=-1), L0_ffn_gate_w, L0_ffn_up_w, L0_ffn_down_w, L0_ffn_gate_s, L0_ffn_up_s, L0_ffn_down_s)
    return x

_drawn_inputs = setup_inputs


def setup_inputs(seed=0):
    import zlib

    import numpy as np

    out = dict(_drawn_inputs(seed))
    spreads = {}
    factors = {}
    for name, (base, spread) in spreads.items():
        noise = np.random.default_rng([zlib.crc32(name.encode()), seed]).standard_normal(out[name].shape)
        drawn = base * np.exp(spread * noise) if base else spread * noise
        out[name] = jnp.asarray(drawn.astype(out[name].dtype))
    for name, factor in factors.items():
        out[name] = (out[name] * factor).astype(out[name].dtype)
    return out
```

```python
from contextlib import ExitStack

import concourse.bass as bass
from concourse import mybir

ALU = mybir.AluOpType
ACT = mybir.ActivationFunctionType
F32 = mybir.dt.float32
F32R = mybir.dt.float32r
I32 = mybir.dt.int32
AX_X = mybir.AxisListType.X

P = 128
B, T, C = 16, 128, 256
INTER = 704
CC = C // P
UB = 2
UT = UB * T
UNITS = B // UB
GU = 2
GT = GU * UT
GROUPS = UNITS // GU
SEG = CC * UB
PITCH = T + 1
FULL = INTER // P
REST = INTER - FULL * P
MC = FULL + 1
GUC = 2 * FULL + 1
EPS = 1e-5
F_MAX = 70.0
V_TD, V_TF, V_GS, V_US, V_DS = 0, CC, 2 * CC, 2 * CC + MC, 2 * CC + 2 * MC
V_N = V_DS + CC
assert 2 * REST == P and GT == 512


def build(nc, x_tok, x_ch, v_ch, w_gu, w_d, vecs, out_ch):
    with ExitStack() as ctx:
        def sb(name, shape, dt=F32):
            return ctx.enter_context(nc.sbuf_tensor(name, shape, dt))

        def psum(name, shape):
            return ctx.enter_context(nc.psum_tensor(name, shape, F32))

        def sem(name):
            return ctx.enter_context(nc.semaphore(name))

        xt = sb("xt", [P, B, C])
        xc = sb("xc", [P, CC, B * T])
        vc = sb("vc", [P, CC, B * T])
        wgu = sb("wgu", [P, CC * GUC * P])
        wgu_hi = sb("wgu_hi", [P, CC, GUC, P], F32R)
        wgu_lo = sb("wgu_lo", [P, CC, GUC, P], F32R)
        wd = sb("wd", [P, MC * C])
        wd_hi = sb("wd_hi", [P, MC, C], F32R)
        wd_lo = sb("wd_lo", [P, MC, C], F32R)
        vec = sb("vec", [P, V_N])
        ident = sb("ident", [P, P])
        ones = sb("ones", [P, 1])
        mhalf = sb("mhalf", [P, UB])
        decay = sb("decay", [P, SEG, PITCH])
        edc = sb("edc", [P, CC])
        dcol = sb("dcol", [P, CC])
        tfc = sb("tfc", [P, CC])
        nsc = sb("nsc", [P, CC])
        fcol = sb("fcol", [P, CC])
        wany = sb("wany", [P, 2])
        flag = sb("flag", [1, 1], I32)
        st1 = sb("st1", [P, UB, 6])
        mv1 = sb("mv1", [P, 2, UB, 2])
        ve1 = sb("ve1", [P, 2, UB])
        rs1 = sb("rs1", [P, 2, UB])
        kn = sb("kn", [P, 2, UB, C])
        ek = sb("ek", [P, 2, SEG, PITCH])
        pk = sb("pk", [P, 2, SEG, PITCH])
        sa = sb("sa", [P, SEG, PITCH])
        sbb = sb("sbb", [P, SEG, PITCH])
        num = sb("num", [P, 2, SEG, T])
        den = sb("den", [P, 2, SEG, T])
        lden = sb("lden", [P, SEG, T])
        rden = sb("rden", [P, 2, SEG, T])
        yk = sb("yk", [P, SEG, T])
        st2 = sb("st2", [P, UB, 6])
        mv2 = sb("mv2", [P, UB, 2])
        ve2 = sb("ve2", [P, UB])
        rs2 = sb("rs2", [P, UB])
        nb2 = sb("nb2", [P, UB])
        nt = sb("nt", [P, UB, C])
        xh = sb("xh", [P, 2, CC, GT], F32R)
        xl = sb("xl", [P, 2, CC, GT], F32R)
        sil = sb("sil", [P, 2, GT])
        h = sb("h", [P, 2, GT])
        hh = sb("hh", [P, FULL, GT], F32R)
        hl = sb("hl", [P, FULL, GT], F32R)
        hx = sb("hx", [P, GT], F32R)

        ps_k = psum("ps_k", [P, CC, UB, T])
        ps_x = psum("ps_x", [P, 512])
        ps_f = psum("ps_f", [P, 2, 2, GT])
        ps_d = psum("ps_d", [P, CC, GT])

        s_vec = sem("s_vec")
        s_xt = [sem(f"s_xt{g}") for g in range(GROUPS)]
        s_xc = [sem(f"s_xc{g}") for g in range(GROUPS)]
        s_vc = [sem(f"s_vc{g}") for g in range(GROUPS)]
        s_wgu, s_wd = sem("s_wgu"), sem("s_wd")
        s_out = sem("s_out")
        s_const = sem("s_const")
        s_ident = sem("s_ident")
        s_ones = sem("s_ones")
        s_zero = sem("s_zero")
        s_edc, s_dcol, s_tfc, s_f = sem("s_edc"), sem("s_dcol"), sem("s_tfc"), sem("s_f")
        s_decay = sem("s_decay")
        s_whi = sem("s_whi")
        s_wany, s_wcnt, s_flag = (sem(n) for n in ("s_wany", "s_wcnt", "s_flag"))
        s_wlo = sem("s_wlo")
        s_st1, s_mv1, s_ve1, s_rs1, s_kn = (sem(n) for n in ("s_st1", "s_mv1", "s_ve1", "s_rs1", "s_kn"))
        s_kT, s_ek, s_pk, s_pad = (sem(n) for n in ("s_kT", "s_ek", "s_pk", "s_pad"))
        s_sb, s_sa, s_den, s_num, s_ln, s_rd, s_yk, s_x1 = (sem(n) for n in (
            "s_sb", "s_sa", "s_den", "s_num", "s_ln", "s_rd", "s_yk", "s_x1"))
        s_x1T, s_st2, s_mv2, s_ve2, s_rs2, s_nb2, s_nt, s_nT, s_xh, s_xl = (sem(n) for n in (
            "s_x1T", "s_st2", "s_mv2", "s_ve2", "s_rs2", "s_nb2", "s_nt", "s_nT", "s_xh", "s_xl"))
        s_gu, s_sil, s_h, s_hh, s_hl, s_dn = (sem(n) for n in ("s_gu", "s_sil", "s_h", "s_hh", "s_hl", "s_dn"))
        s_hx = sem("s_hx")
        s_fin = sem("s_fin")

        def unit_cols(u):
            return slice(u * UT, (u + 1) * UT)

        def unit_view(t, u):
            return t[:, :, unit_cols(u)].rearrange("p c (b t) -> p c b t", t=T)

        def seqs(t):
            return t.rearrange("p (c b) t -> p c b t", c=CC)

        block = ctx.enter_context(nc.Block())

        @block.sync
        def _(sp):
            def load_group(g):
                bs = slice(g * GU * UB, (g + 1) * GU * UB)
                ts = slice(g * GT, (g + 1) * GT)
                sp.dma_start(xt[:, bs, :], x_tok[bs, :, :].rearrange("b t c -> t b c")).then_inc(s_xt[g], 16)
                sp.dma_start(vc[:, :, ts], v_ch[:, ts].rearrange("(k p) n -> p k n", p=P)).then_inc(s_vc[g], 16)
                sp.dma_start(xc[:, :, ts], x_ch[:, ts].rearrange("(k p) n -> p k n", p=P)).then_inc(s_xc[g], 16)

            sp.dma_start(vec[:, :], vecs).then_inc(s_vec, 16)
            load_group(0)
            sp.dma_start(wgu[:, :], w_gu).then_inc(s_wgu, 16)
            sp.dma_start(wd[:, :], w_d).then_inc(s_wd, 16)
            for g in range(1, GROUPS):
                load_group(g)
            for g in range(GROUPS):
                for c in range(CC):
                    sp.wait_ge(s_fin, CC * g + c + 1)
                    sp.dma_start(out_ch[c * P:(c + 1) * P, g * GT:(g + 1) * GT],
                                 xc[:, c, g * GT:(g + 1) * GT]).then_inc(s_out, 16)
            sp.wait_ge(s_out, 16 * GROUPS * CC)

        @block.gpsimd
        def _(pool):
            nc.gpsimd.memset(mhalf[:, :], -0.5).then_inc(s_const, 1)
            nc.gpsimd.memset(ident[:, :], 0.0).then_inc(s_const, 1)
            pool.wait_ge(s_const, 2)
            nc.gpsimd.affine_select(out=ident[:, :], in_=ident[:, :], compare_op=ALU.not_equal, fill=1.0,
                                    base=0, pattern=[[-1, P]], channel_multiplier=1).then_inc(s_ident, 1)

            def rstd1(u):
                pool.wait_ge(s_ve1, u + 1)
                if u >= 2:
                    pool.wait_ge(s_kn, u - 1)
                nc.gpsimd.tensor_tensor(rs1[:, u % 2, :], ve1[:, u % 2, :], mhalf[:, :], ALU.pow).then_inc(s_rs1, 1)

            def weigh(u):
                pool.wait_ge(s_ek, u + 1)
                if u % GU == 0:
                    pool.wait_ge(s_vc[u // GU], 16)
                if u >= 2:
                    pool.wait_ge(s_num, u - 1)
                v = vc[:, :, unit_cols(u)].rearrange("p c (b t) -> p c b t", t=T)
                nc.gpsimd.tensor_tensor(seqs(pk[:, u % 2, :, 1:PITCH]), seqs(ek[:, u % 2, :, 1:PITCH]), v,
                                        ALU.mult).then_inc(s_pk, 1)

            def mix(u):
                pool.wait_ge(s_num, u + 1)
                pool.wait_ge(s_rd, u + 1)
                if u >= 1:
                    pool.wait_ge(s_x1, u)
                nc.gpsimd.tensor_tensor(yk[:, :, :], num[:, u % 2, :, :], rden[:, u % 2, :, :],
                                        ALU.mult).then_inc(s_yk, 1)
                if u % GU == 0:
                    pool.wait_ge(s_xc[u // GU], 16)
                pool.wait_ge(s_yk, u + 1)
                nc.gpsimd.tensor_tensor(unit_view(xc, u), unit_view(xc, u), seqs(yk[:, :, :]),
                                        ALU.add).then_inc(s_x1, 1)

            def rstd2(u):
                pool.wait_ge(s_ve2, u + 1)
                if u >= 1:
                    pool.wait_ge(s_nt, u)
                nc.gpsimd.tensor_tensor(rs2[:, :], ve2[:, :], mhalf[:, :], ALU.pow).then_inc(s_rs2, 1)

            def low(g, m):
                n = MC * g + m
                pool.wait_ge(s_hh, n + 1)
                if g >= 1:
                    pool.wait_ge(s_dn, n - MC + 1)
                nc.gpsimd.tensor_tensor(hl[:, m, :], h[:, m % 2, :], hh[:, m, :].bitcast(F32),
                                        ALU.subtract).then_inc(s_hl, 1)

            def weights_low():
                pool.wait_ge(s_flag, 1)
                found = pool.value_load(flag[0:1, 0:1], min_val=0, max_val=P * (CC * GUC * P + MC * C))
                pool.wait_ge(s_whi, 2)
                with pool.If(found > 0):
                    for raw, hi, lo in ((wgu[:, :], wgu_hi[:, :, :, :].rearrange("p c m n -> p (c m n)"),
                                         wgu_lo[:, :, :, :].rearrange("p c m n -> p (c m n)")),
                                        (wd[:, :], wd_hi[:, :, :].rearrange("p m n -> p (m n)"),
                                         wd_lo[:, :, :].rearrange("p m n -> p (m n)"))):
                        nc.gpsimd.tensor_tensor(lo, raw, hi.bitcast(F32), ALU.subtract).then_inc(s_wlo, 1)
                with pool.Else():
                    pool.nop()

            PLAN.gpsimd(weights_low=weights_low, rstd1=rstd1, weigh=weigh, mix=mix, rstd2=rstd2, low=low)

        @block.scalar
        def _(act):
            act.wait_ge(s_vec, 16)
            nc.scalar.activation(edc[:, :], vec[:, V_TD:V_TD + CC], ACT.Exp).then_inc(s_edc, 1)
            act.wait_ge(s_edc, 1)
            nc.scalar.activation(dcol[:, :], edc[:, :], ACT.Exp, scale=-1.0).then_inc(s_dcol, 1)
            act.wait_ge(s_tfc, 2)
            nc.scalar.activation(fcol[:, :], tfc[:, :], ACT.Exp).then_inc(s_f, 1)

            def expk(u):
                act.wait_ge(s_kT, u + 1)
                if u >= 2:
                    act.wait_ge(s_num, u - 1)
                for c in range(CC):
                    last = nc.scalar.activation(ek[:, u % 2, c * UB:(c + 1) * UB, 1:PITCH], ps_k[:, c, :, :],
                                                ACT.Exp, bias=nsc[:, c:c + 1])
                last.then_inc(s_ek, 1)

            def recip(u):
                act.wait_ge(s_den, u + 1)
                if u >= 1:
                    act.wait_ge(s_rd, u)
                nc.scalar.activation(lden[:, :, :], den[:, u % 2, :, :], ACT.Ln).then_inc(s_ln, 1)
                act.wait_ge(s_ln, u + 1)
                if u >= 2:
                    act.wait_ge(s_yk, u - 1)
                nc.scalar.activation(rden[:, u % 2, :, :], lden[:, :, :], ACT.Exp, scale=-1.0).then_inc(s_rd, 1)

            def norm2(u):
                act.wait_ge(s_nb2, u + 1)
                if u >= 1:
                    act.wait_ge(s_nT, u)
                for b in range(UB):
                    last = nc.scalar.activation(nt[:, b, :], ps_x[:, b * C:(b + 1) * C], ACT.Identity,
                                                scale=rs2[:, b:b + 1], bias=nb2[:, b:b + 1])
                last.then_inc(s_nt, 1)

            def high_n(u):
                g = u // GU
                act.wait_ge(s_nT, u + 1)
                if g >= 2:
                    act.wait_ge(s_gu, MC * (g - 1))
                o = (u % GU) * UT
                nc.scalar.activation(xh[:, g % 2, :, o:o + UT], ps_x[:, :].rearrange("p (c n) -> p c n", c=CC),
                                     ACT.Copy).then_inc(s_xh, 1)

            def silu(g, m):
                n = MC * g + m
                act.wait_ge(s_gu, n + 1)
                if n >= 2:
                    act.wait_ge(s_h, n - 1)
                if m < FULL:
                    nc.scalar.activation(sil[:, m % 2, :], ps_f[:, m % 2, 0, :], ACT.Silu,
                                         scale=vec[:, V_GS + m:V_GS + m + 1]).then_inc(s_sil, 1)
                else:
                    nc.scalar.activation(sil[REST:P, m % 2, :], ps_f[0:REST, m % 2, 0, :], ACT.Silu,
                                         scale=vec[0:REST, V_GS + m:V_GS + m + 1]).then_inc(s_sil, 1)

            def high_h(g, m):
                n = MC * g + m
                act.wait_ge(s_h, n + 1)
                if g >= 1:
                    act.wait_ge(s_dn, n - MC + 1)
                if m < FULL:
                    nc.scalar.activation(hh[:, m, :], h[:, m % 2, :], ACT.Copy).then_inc(s_hh, 1)
                else:
                    nc.scalar.activation(hx[REST:P, :], h[REST:P, m % 2, :], ACT.Copy).then_inc(s_hh, 1)

            PLAN.scalar(expk=expk, recip=recip, norm2=norm2, high_n=high_n, silu=silu, high_h=high_h)

        @block.vector
        def _(dve):
            nc.vector.memset(decay[:, :, :], 0.0).then_inc(s_zero, 1)
            nc.vector.memset(ones[:, :], 1.0).then_inc(s_ones, 1)
            dve.wait_ge(s_vec, 16)
            nc.vector.tensor_scalar(tfc[:, :], vec[:, V_TF:V_TF + CC], F_MAX, None, ALU.min).then_inc(s_tfc, 1)
            dve.wait_ge(s_tfc, 1)
            nc.vector.tensor_scalar(nsc[:, :], tfc[:, :], 0.0, -1.0, ALU.max, ALU.mult).then_inc(s_tfc, 1)

            def decay_tile():
                dve.wait_ge(s_zero, 1)
                dve.wait_ge(s_dcol, 1)
                for c in range(CC):
                    cols = decay[:, c * UB:(c + 1) * UB, 2:PITCH]
                    last = nc.vector.tensor_scalar(cols, cols, dcol[:, c:c + 1], None, ALU.add)
                last.then_inc(s_decay, 1)

            def weights_high(k):
                dve.wait_ge((s_wgu, s_wd)[k], 16)
                dst = (wgu_hi[:, :, :, :].rearrange("p c m n -> p (c m n)"), wd_hi[:, :, :].rearrange("p m n -> p (m n)"))[k]
                nc.vector.tensor_copy(dst, (wgu, wd)[k][:, :]).then_inc(s_whi, 1)

            def weights_check():
                dve.wait_ge(s_whi, 2)
                for k, (w, hi, lo) in enumerate((
                        (wgu[:, :], wgu_hi[:, :, :, :].rearrange("p c m n -> p (c m n)"),
                         wgu_lo[:, :, :, :].rearrange("p c m n -> p (c m n)")),
                        (wd[:, :], wd_hi[:, :, :].rearrange("p m n -> p (m n)"),
                         wd_lo[:, :, :].rearrange("p m n -> p (m n)")))):
                    nc.vector.scalar_tensor_tensor(lo, w, 0.0, hi.bitcast(F32), ALU.bypass, ALU.not_equal,
                                                   accum_out=wany[:, k:k + 1]).then_inc(s_wany, 1)

            def publish():
                dve.wait_ge(s_wcnt, 1)
                nc.vector.tensor_copy(flag[:, :], ps_d[0:1, 0, 0:1]).then_inc(s_flag, 1)

            def stats1(u):
                if u % GU == 0:
                    dve.wait_ge(s_xt[u // GU], 16)
                if u >= 1:
                    dve.wait_ge(s_mv1, u)
                for b in range(UB):
                    last = nc.vector.bn_stats(st1[:, b, :], xt[:, u * UB + b, :])
                last.then_inc(s_st1, 1)
                dve.wait_ge(s_st1, u + 1)
                for b in range(UB):
                    last = nc.vector.bn_aggr(mv1[:, u % 2, b, :], st1[:, b, :])
                last.then_inc(s_mv1, 1)
                dve.wait_ge(s_mv1, u + 1)
                if u >= 2:
                    dve.wait_ge(s_rs1, u - 1)
                nc.vector.tensor_scalar(ve1[:, u % 2, :], mv1[:, u % 2, :, 1], EPS, None, ALU.add).then_inc(s_ve1, 1)

            def norm1(u):
                dve.wait_ge(s_rs1, u + 1)
                if u >= 2:
                    dve.wait_ge(s_kT, u - 1)
                for b in range(UB):
                    last = nc.vector.tensor_scalar(kn[:, u % 2, b, :], xt[:, u * UB + b, :], mv1[:, u % 2, b, 0:1],
                                                   rs1[:, u % 2, b:b + 1], ALU.subtract, ALU.mult)
                last.then_inc(s_kn, 1)

            def scan(u):
                s = u % 2
                dve.wait_ge(s_ek, u + 1)
                nc.vector.tensor_copy(ek[:, s, :, 0:1], ek[:, s, :, 1:2]).then_inc(s_pad, 1)
                dve.wait_ge(s_pk, u + 1)
                nc.vector.tensor_copy(pk[:, s, :, 0:1], pk[:, s, :, 1:2]).then_inc(s_pad, 1)
                if u == 0:
                    dve.wait_ge(s_decay, 1)
                else:
                    dve.wait_ge(s_num, u)
                dve.wait_ge(s_pad, 2 * u + 2)
                flat = [t.rearrange("p q t -> p (q t)") for t in (sbb[:, :, :], sa[:, :, :], decay[:, :, :],
                                                                  ek[:, s, :, :], pk[:, s, :, :])]
                nc.vector.tensor_tensor_scan(flat[0], flat[2], flat[3], 0.0, ALU.mult, ALU.add).then_inc(s_sb, 1)
                nc.vector.tensor_tensor_scan(flat[1], flat[2], flat[4], 0.0, ALU.mult, ALU.add).then_inc(s_sa, 1)

            def ratio(u):
                s = u % 2
                if u == 0:
                    dve.wait_ge(s_f, 1)
                if u >= 2:
                    dve.wait_ge(s_ln, u - 1)
                dve.wait_ge(s_sb, u + 1)
                for c in range(CC):
                    q = slice(c * UB, (c + 1) * UB)
                    last = nc.vector.scalar_tensor_tensor(den[:, s, q, :], ek[:, s, q, 1:PITCH], fcol[:, c:c + 1],
                                                          sbb[:, q, 0:T], ALU.mult, ALU.add)
                last.then_inc(s_den, 1)
                if u >= 2:
                    dve.wait_ge(s_yk, u - 1)
                dve.wait_ge(s_sa, u + 1)
                dve.wait_ge(s_den, u + 1)
                for c in range(CC):
                    q = slice(c * UB, (c + 1) * UB)
                    last = nc.vector.scalar_tensor_tensor(num[:, s, q, :], pk[:, s, q, 1:PITCH], fcol[:, c:c + 1],
                                                          sa[:, q, 0:T], ALU.mult, ALU.add)
                last.then_inc(s_num, 1)

            def stats2(u):
                dve.wait_ge(s_x1T, u + 1)
                if u >= 1:
                    dve.wait_ge(s_mv2, u)
                for b in range(UB):
                    last = nc.vector.bn_stats(st2[:, b, :], ps_x[:, b * C:(b + 1) * C])
                last.then_inc(s_st2, 1)
                dve.wait_ge(s_st2, u + 1)
                if u >= 1:
                    dve.wait_ge(s_nb2, u)
                for b in range(UB):
                    last = nc.vector.bn_aggr(mv2[:, b, :], st2[:, b, :])
                last.then_inc(s_mv2, 1)
                dve.wait_ge(s_mv2, u + 1)
                if u >= 1:
                    dve.wait_ge(s_rs2, u)
                nc.vector.tensor_scalar(ve2[:, :], mv2[:, :, 1], EPS, None, ALU.add).then_inc(s_ve2, 1)

            def bias2(u):
                dve.wait_ge(s_rs2, u + 1)
                if u >= 1:
                    dve.wait_ge(s_nt, u)
                nc.vector.scalar_tensor_tensor(nb2[:, :], mv2[:, :, 0], -1.0, rs2[:, :], ALU.mult,
                                               ALU.mult).then_inc(s_nb2, 1)

            def low_n(u):
                g = u // GU
                dve.wait_ge(s_xh, u + 1)
                if g >= 2:
                    dve.wait_ge(s_gu, MC * (g - 1))
                o = (u % GU) * UT
                nc.vector.tensor_tensor(xl[:, g % 2, :, o:o + UT], ps_x[:, :].rearrange("p (c n) -> p c n", c=CC),
                                        xh[:, g % 2, :, o:o + UT].bitcast(F32), ALU.subtract).then_inc(s_xl, 1)

            def gated(g, m):
                n = MC * g + m
                dve.wait_ge(s_sil, n + 1)
                if n >= 2:
                    dve.wait_ge(s_hh, n - 1)
                    if (n - 2) % MC < FULL:
                        dve.wait_ge(s_hl, (n - 2) // MC * FULL + (n - 2) % MC + 1)
                r = slice(0, P) if m < FULL else slice(REST, P)
                part = 1 if m < FULL else 0
                nc.vector.scalar_tensor_tensor(h[r, m % 2, :], ps_f[r, m % 2, part, :], vec[r, V_US + m:V_US + m + 1],
                                               sil[r, m % 2, :], ALU.mult, ALU.mult).then_inc(s_h, 1)

            def low_rest(g):
                n = MC * g + FULL
                dve.wait_ge(s_hh, n + 1)
                if g >= 1:
                    dve.wait_ge(s_dn, n - MC + 1)
                nc.vector.tensor_tensor(hx[0:REST, :], h[REST:P, FULL % 2, :], hx[REST:P, :].bitcast(F32),
                                        ALU.subtract).then_inc(s_hx, 1)

            def finish(g):
                dve.wait_ge(s_dn, MC * (g + 1))
                dve.wait_ge(s_x1, GU * (g + 1))
                ts = slice(g * GT, (g + 1) * GT)
                for c in range(CC):
                    nc.vector.scalar_tensor_tensor(xc[:, c, ts], ps_d[:, c, :], vec[:, V_DS + c:V_DS + c + 1],
                                                   xc[:, c, ts], ALU.mult, ALU.add).then_inc(s_fin, 1)

            PLAN.vector(decay_tile=decay_tile, weights_high=weights_high, weights_check=weights_check, publish=publish, stats1=stats1,
                        norm1=norm1, scan=scan, ratio=ratio, stats2=stats2, bias2=bias2, low_n=low_n, gated=gated,
                        low_rest=low_rest, finish=finish)

        @block.tensor
        def _(pe):
            def k_T(u):
                pe.wait_ge(s_kn, u + 1)
                if u == 0:
                    pe.wait_ge(s_ident, 1)
                else:
                    pe.wait_ge(s_ek, u)
                for b in range(UB):
                    for c in range(CC):
                        last = nc.tensor.transpose(ps_k[:, c, b, :], kn[:, u % 2, b, c * P:(c + 1) * P], ident[:, :])
                last.then_inc(s_kT, 1)

            def x1_T(u):
                pe.wait_ge(s_x1, u + 1)
                if u >= 1:
                    pe.wait_ge(s_xl, u)
                for b in range(UB):
                    for c in range(CC):
                        t0 = u * UT + b * T
                        last = nc.tensor.transpose(ps_x[:, b * C + c * P:b * C + (c + 1) * P], xc[:, c, t0:t0 + T],
                                                   ident[:, :])
                last.then_inc(s_x1T, 1)

            def n_T(u):
                pe.wait_ge(s_nt, u + 1)
                for b in range(UB):
                    for c in range(CC):
                        last = nc.tensor.transpose(ps_x[:, c * UT + b * T:c * UT + (b + 1) * T],
                                                   nt[:, b, c * P:(c + 1) * P], ident[:, :])
                last.then_inc(s_nT, 1)

            def gate_up(g, m, weights):
                n = MC * g + m
                if m == 0:
                    pe.wait_ge(s_xl, GU * (g + 1))
                if n >= 2:
                    pe.wait_ge(s_h, n - 1)
                for part, tile in (((0, m), (1, FULL + m)) if m < FULL else ((0, 2 * FULL),)):
                    todo = [(w, c, x) for w in weights for c in range(CC) for x in (xh, xl)]
                    for i, (w, c, x) in enumerate(todo):
                        last = nc.tensor.matmul(ps_f[:, m % 2, part, :], w[0][:, c, tile, :], x[:, g % 2, c, :],
                                                start=i == 0, stop=i == len(todo) - 1)
                last.then_inc(s_gu, 1)

            def down(g, m, weights):
                n = MC * g + m
                if m == 0 and g >= 1:
                    pe.wait_ge(s_fin, CC * g)
                if m < FULL:
                    pe.wait_ge(s_hl, FULL * g + m + 1)
                else:
                    pe.wait_ge(s_hx, g + 1)
                for c in range(CC):
                    todo = [(w, a) for w in weights for a in ((hh[:, m, :], hl[:, m, :]) if m < FULL else (hx[:, :],))]
                    for i, (w, a) in enumerate(todo):
                        last = nc.tensor.matmul(ps_d[:, c, :], w[1][:, m, c * P:(c + 1) * P], a,
                                                start=m == 0 and i == 0, stop=m == MC - 1 and i == len(todo) - 1)
                last.then_inc(s_dn, 1)

            def count():
                pe.wait_ge(s_ones, 1)
                pe.wait_ge(s_wany, 2)
                nc.tensor.matmul(ps_d[0:1, 0, 0:1], ones[:, :], wany[:, 0:1], start=True, stop=False)
                nc.tensor.matmul(ps_d[0:1, 0, 0:1], ones[:, :], wany[:, 1:2], start=False, stop=True).then_inc(s_wcnt, 1)

            def iteration(g, weights):
                PLAN.tensor(g, weights, k_T=k_T, x1_T=x1_T, n_T=n_T, gate_up=gate_up, down=down, count=count)

            high = (wgu_hi, wd_hi)
            k_T(0)
            iteration(-2, None)
            iteration(-1, None)
            pe.wait_ge(s_whi, 2)
            pe.wait_ge(s_flag, 1)
            found = pe.value_load(flag[0:1, 0:1], min_val=0, max_val=P * (CC * GUC * P + MC * C))
            with pe.If(found > 0):
                pe.wait_ge(s_wlo, 2)
                for g in range(GROUPS):
                    iteration(g, [high, (wgu_lo, wd_lo)])
            with pe.Else():
                for g in range(GROUPS):
                    iteration(g, [high])
            pe.nop()


class PLAN:

    @staticmethod
    def units(g):
        return [GU * g + i for i in range(GU)] if 0 <= g < GROUPS else [None] * GU

    @staticmethod
    def gpsimd(weights_low, rstd1, weigh, mix, rstd2, low):
        def on(f, *a):
            if a[0] is not None:
                f(*a)
        rstd1(0)
        rstd1(1)
        for g in range(-2, GROUPS):
            r0, r1 = PLAN.units(g + 2)
            l0, l1 = PLAN.units(g + 1)
            n0, n1 = PLAN.units(g + 3)
            ff = g if g >= 0 else None
            on(mix, l0)
            on(weigh, r0)
            on(mix, l1)
            on(weigh, r1)
            if ff is not None:
                low(g, 0)
            on(rstd2, l0)
            if ff is not None:
                low(g, 1)
                low(g, 2)
            on(rstd2, l1)
            if ff is not None:
                low(g, 3)
            on(rstd1, n0)
            if ff is not None:
                low(g, 4)
            on(rstd1, n1)
            if g == -1:
                weights_low()

    @staticmethod
    def scalar(expk, recip, norm2, high_n, silu, high_h):
        def on(f, *a):
            if a[0] is not None:
                f(*a)
        for g in range(-2, GROUPS):
            r0, r1 = PLAN.units(g + 2)
            l0, l1 = PLAN.units(g + 1)
            on(expk, r0)
            on(recip, l0)
            on(expk, r1)
            on(recip, l1)
            ff = g >= 0
            if ff:
                silu(g, 0)
                silu(g, 1)
                high_h(g, 0)
            on(norm2, l0)
            if ff:
                silu(g, 2)
                high_h(g, 1)
            on(high_n, l0)
            if ff:
                silu(g, 3)
                high_h(g, 2)
            on(norm2, l1)
            if ff:
                silu(g, 4)
                high_h(g, 3)
            on(high_n, l1)
            if ff:
                silu(g, 5)
                high_h(g, 4)
                high_h(g, 5)

    @staticmethod
    def vector(decay_tile, weights_high, weights_check, publish, stats1, norm1, scan, ratio, stats2, bias2, low_n, gated,
               low_rest, finish):
        def on(f, *a):
            if a[0] is not None:
                f(*a)
        stats1(0)
        stats1(1)
        norm1(0)
        norm1(1)
        decay_tile()
        for g in range(-2, GROUPS):
            r0, r1 = PLAN.units(g + 2)
            l0, l1 = PLAN.units(g + 1)
            n0, n1 = PLAN.units(g + 3)
            ff = g >= 0
            if ff:
                gated(g, 0)
            on(scan, r0)
            if ff:
                gated(g, 1)
            on(ratio, r0)
            on(stats2, l0)
            on(scan, r1)
            on(bias2, l0)
            if ff:
                gated(g, 2)
            on(ratio, r1)
            on(low_n, l0)
            if g == -1:
                publish()
            if ff:
                gated(g, 3)
            on(stats2, l1)
            on(stats1, n0)
            on(bias2, l1)
            on(stats1, n1)
            if ff:
                gated(g, 4)
            if g == -2:
                weights_high(0)
                weights_high(1)
                weights_check()
            on(norm1, n0)
            on(low_n, l1)
            on(norm1, n1)
            if ff:
                gated(g, 5)
                low_rest(g)
                finish(g)

    @staticmethod
    def tensor(g, weights, k_T, x1_T, n_T, gate_up, down, count):
        def on(f, *a):
            if a[0] is not None:
                f(*a)
        r0, r1 = PLAN.units(g + 2)
        l0, l1 = PLAN.units(g + 1)
        n0, n1 = PLAN.units(g + 3)
        ff = g >= 0
        on(k_T, r1)
        if ff:
            gate_up(g, 0, weights)
            gate_up(g, 1, weights)
        on(x1_T, l0)
        if ff:
            gate_up(g, 2, weights)
            down(g, 0, weights)
        on(n_T, l0)
        if g == -1:
            count()
        if ff:
            gate_up(g, 3, weights)
            down(g, 1, weights)
        on(x1_T, l1)
        if ff:
            gate_up(g, 4, weights)
            down(g, 2, weights)
        on(n_T, l1)
        if ff:
            gate_up(g, 5, weights)
            down(g, 3, weights)
            down(g, 4, weights)
        on(k_T, n0)
        if ff:
            down(g, 5, weights)


def kernel(x, ctx_2048, L0_xattn_time_decay, L0_xattn_time_first, L0_ffn_gate_w, L0_ffn_up_w, L0_ffn_down_w,
           L0_ffn_gate_s, L0_ffn_up_s, L0_ffn_down_s):
    import numpy as np
    import concourse.bacc as bacc
    from concourse.bass_utils import run_bass_kernel_spmd

    x, v = np.asarray(x), np.asarray(ctx_2048)
    cut = FULL * P

    def tiles(w, n):
        return w.reshape(n, P, -1).transpose(1, 0, 2)

    gT, uT = np.asarray(L0_ffn_gate_w).T, np.asarray(L0_ffn_up_w).T
    gu = np.concatenate([gT[:, :cut], uT[:, :cut], gT[:, cut:], uT[:, cut:]], axis=1)
    dT = np.asarray(L0_ffn_down_w).T
    dT = np.concatenate([dT[:cut], dT[cut:], dT[cut:]], axis=0)
    gs, us = np.asarray(L0_ffn_gate_s), np.asarray(L0_ffn_up_s)
    cols = [np.asarray(L0_xattn_time_decay), np.asarray(L0_xattn_time_first), np.concatenate([gs, gs[cut:]]),
            np.concatenate([us, us[cut:]]), np.asarray(L0_ffn_down_s)]
    arrays = {
        "x_tok": x,
        "x_ch": x.reshape(B * T, C).T,
        "v_ch": v.reshape(B * T, C).T,
        "w_gu": tiles(gu, CC).reshape(P, CC * GUC * P),
        "w_d": tiles(dT, MC).reshape(P, MC * C),
        "vecs": np.concatenate([a.reshape(-1, P) for a in cols], axis=0).T,
    }
    arrays = {k: np.ascontiguousarray(a) for k, a in arrays.items()}
    nc = bacc.Bacc("TRN2", target_bir_lowering=False, num_devices=1)
    args = [nc.dram_tensor(k, a.shape, F32, kind="ExternalInput").ap() for k, a in arrays.items()]
    out = nc.dram_tensor("out_ch", (C, B * T), F32, kind="ExternalOutput").ap()
    build(nc, *args, out)
    r = run_bass_kernel_spmd(nc, [arrays], core_ids=[0])
    return np.ascontiguousarray(r.results[0]["out_ch"].T).reshape(B, T, C)
```

```python
from contextlib import ExitStack

import concourse.bass as bass
from concourse import mybir

ALU = mybir.AluOpType
ACT = mybir.ActivationFunctionType
F32 = mybir.dt.float32
F32R = mybir.dt.float32r
I32 = mybir.dt.int32
AX_X = mybir.AxisListType.X

P = 128
B, T, C = 16, 128, 256
INTER = 704
CC = C // P
UB = 2
UT = UB * T
UNITS = B // UB
GU = 2
GT = GU * UT
GROUPS = UNITS // GU
SEG = CC * UB
PITCH = T + 1
FULL = INTER // P
REST = INTER - FULL * P
MC = FULL + 1
GUC = 2 * FULL + 1
EPS = 1e-5
F_MAX = 70.0
V_TD, V_TF, V_GS, V_US, V_DS = 0, CC, 2 * CC, 2 * CC + MC, 2 * CC + 2 * MC
V_N = V_DS + CC
EARLY = 2
HS = 3
LN_EXP, SILU = "natural_log_exp_and_others", "silu_and_others"
W_SIZES = (CC * GUC * P, MC * C)
PIECES_OF = (4, 3)
PIECES = [(k, i * (W_SIZES[k] // n), W_SIZES[k] // n) for k, n in enumerate(PIECES_OF) for i in range(n)]
assert 2 * REST == P and GT == 512


def build(nc, x_tok, x_ch, v_ch, w_gu, w_d, vecs, out_ch):
    with ExitStack() as ctx:
        def sb(name, shape, dt=F32):
            return ctx.enter_context(nc.sbuf_tensor(name, shape, dt))

        def psum(name, shape):
            return ctx.enter_context(nc.psum_tensor(name, shape, F32))

        def sem(name):
            return ctx.enter_context(nc.semaphore(name))

        xt = sb("xt", [P, B, C])
        xc = sb("xc", [P, CC, B * T])
        vc = sb("vc", [P, CC, B * T])
        wgu = sb("wgu", [P, CC * GUC * P])
        wgu_hi = sb("wgu_hi", [P, CC, GUC, P], F32R)
        wgu_lo = sb("wgu_lo", [P, CC, GUC, P], F32R)
        wd = sb("wd", [P, MC * C])
        wd_hi = sb("wd_hi", [P, MC, C], F32R)
        wd_lo = sb("wd_lo", [P, MC, C], F32R)
        vec = sb("vec", [P, V_N])
        ident = sb("ident", [P, P])
        ones = sb("ones", [P, 1])
        mhalf = sb("mhalf", [P, UB])
        decay = sb("decay", [P, SEG, PITCH])
        edc = sb("edc", [P, CC])
        dcol = sb("dcol", [P, CC])
        tfc = sb("tfc", [P, CC])
        nsc = sb("nsc", [P, CC])
        fcol = sb("fcol", [P, CC])
        wsum = sb("wsum", [P, 2])
        wany = sb("wany", [P, 2])
        junk = sb("junk", [P, CC * GUC * P], mybir.dt.bfloat16)
        flag = sb("flag", [1, 1], I32)
        st1 = sb("st1", [P, 2, UB, 6])
        mv1 = sb("mv1", [P, 2, UB, 2])
        ve1 = sb("ve1", [P, 2, UB])
        rs1 = sb("rs1", [P, 2, UB])
        kn = sb("kn", [P, 2, UB, C])
        ek = sb("ek", [P, 2, SEG, PITCH])
        pk = sb("pk", [P, 2, SEG, PITCH])
        sa = sb("sa", [P, 2, SEG, PITCH])
        sbb = sb("sbb", [P, 2, SEG, PITCH])
        num = sb("num", [P, 2, SEG, T])
        den = sb("den", [P, 2, SEG, T])
        lden = sb("lden", [P, 2, SEG, T])
        rden = sb("rden", [P, 2, SEG, T])
        yk = sb("yk", [P, 2, SEG, T])
        st2 = sb("st2", [P, UB, 6])
        mv2 = sb("mv2", [P, UB, 2])
        ve2 = sb("ve2", [P, UB])
        rs2 = sb("rs2", [P, UB])
        nb2 = sb("nb2", [P, UB])
        nt = sb("nt", [P, UB, C])
        xh = sb("xh", [P, 2, CC, GT], F32R)
        xl = sb("xl", [P, 2, CC, GT], F32R)
        sil = sb("sil", [P, 2, GT])
        h = sb("h", [P, HS, GT])
        hh = sb("hh", [P, FULL, GT], F32R)
        hl = sb("hl", [P, FULL, GT], F32R)
        hx = sb("hx", [P, GT], F32R)

        ps_k = psum("ps_k", [P, CC, UB, T])
        ps_x = psum("ps_x", [P, 512])
        ps_f = psum("ps_f", [P, 2, 2, GT])
        ps_d = psum("ps_d", [P, CC, GT])

        s_vec = sem("s_vec")
        s_xt = [sem(f"s_xt{g}") for g in range(GROUPS)]
        s_xc = [sem(f"s_xc{g}") for g in range(GROUPS)]
        s_vc = [sem(f"s_vc{g}") for g in range(GROUPS)]
        s_wgu, s_wd = sem("s_wgu"), sem("s_wd")
        s_out = sem("s_out")
        s_const = sem("s_const")
        s_ident = sem("s_ident")
        s_ones = sem("s_ones")
        s_zero = sem("s_zero")
        s_edc, s_dcol, s_tfc, s_f = sem("s_edc"), sem("s_dcol"), sem("s_tfc"), sem("s_f")
        s_decay = sem("s_decay")
        s_whi = sem("s_whi")
        s_wsum = sem("s_wsum")
        s_wany, s_wcnt, s_flag = (sem(n) for n in ("s_wany", "s_wcnt", "s_flag"))
        s_wlo = sem("s_wlo")
        s_st1, s_mv1, s_ve1, s_rs1 = (sem(n) for n in ("s_st1", "s_mv1", "s_ve1", "s_rs1"))
        s_kT, s_ek, s_pad = (sem(n) for n in ("s_kT", "s_ek", "s_pad"))
        s_kn, s_pk, s_yk, s_x1 = ((sem(n + "_early"), sem(n)) for n in ("s_kn", "s_pk", "s_yk", "s_x1"))
        s_sb, s_sa, s_den, s_num, s_ln, s_rd = (sem(n) for n in ("s_sb", "s_sa", "s_den", "s_num", "s_ln", "s_rd"))
        s_x1T, s_st2, s_mv2, s_ve2, s_rs2, s_nb2, s_nt, s_nT, s_xh, s_xl = (sem(n) for n in (
            "s_x1T", "s_st2", "s_mv2", "s_ve2", "s_rs2", "s_nb2", "s_nt", "s_nT", "s_xh", "s_xl"))
        s_gu, s_sil, s_h, s_hh, s_hl, s_dn = (sem(n) for n in ("s_gu", "s_sil", "s_h", "s_hh", "s_hl", "s_dn"))
        s_hx = sem("s_hx")
        s_fin = sem("s_fin")

        def unit_cols(u):
            return slice(u * UT, (u + 1) * UT)

        def unit_view(t, u):
            return t[:, :, unit_cols(u)].rearrange("p c (b t) -> p c b t", t=T)

        def seqs(t):
            return t.rearrange("p (c b) t -> p c b t", c=CC)

        w_flat = [(wgu[:, :], wgu_hi[:, :, :, :].rearrange("p c m n -> p (c m n)"),
                   wgu_lo[:, :, :, :].rearrange("p c m n -> p (c m n)")),
                  (wd[:, :], wd_hi[:, :, :].rearrange("p m n -> p (m n)"),
                   wd_lo[:, :, :].rearrange("p m n -> p (m n)"))]

        def wait_low(eng, n):
            g, m = divmod(n, MC)
            if m < FULL:
                eng.wait_ge(s_hl, FULL * g + m + 1)
            else:
                eng.wait_ge(s_hx, g + 1)

        block = ctx.enter_context(nc.Block())

        @block.sync
        def _(sp):
            def load_group(g):
                bs = slice(g * GU * UB, (g + 1) * GU * UB)
                ts = slice(g * GT, (g + 1) * GT)
                sp.dma_start(xt[:, bs, :], x_tok[bs, :, :].rearrange("b t c -> t b c")).then_inc(s_xt[g], 16)
                sp.dma_start(vc[:, :, ts], v_ch[:, ts].rearrange("(k p) n -> p k n", p=P)).then_inc(s_vc[g], 16)
                sp.dma_start(xc[:, :, ts], x_ch[:, ts].rearrange("(k p) n -> p k n", p=P)).then_inc(s_xc[g], 16)

            sp.dma_start(vec[:, :], vecs).then_inc(s_vec, 16)
            load_group(0)
            sp.dma_start(wgu[:, :], w_gu).then_inc(s_wgu, 16)
            sp.dma_start(wd[:, :], w_d).then_inc(s_wd, 16)
            for g in range(1, GROUPS):
                load_group(g)
            for g in range(GROUPS):
                for c in range(CC):
                    sp.wait_ge(s_fin, CC * g + c + 1)
                    sp.dma_start(out_ch[c * P:(c + 1) * P, g * GT:(g + 1) * GT],
                                 xc[:, c, g * GT:(g + 1) * GT]).then_inc(s_out, 16)
            sp.wait_ge(s_out, 16 * GROUPS * CC)

        def turn(pair, u):
            return (pair[0], u + 1) if u < EARLY else (pair[1], u - EARLY + 1)

        def wait_turn(eng, pair, u):
            eng.wait_ge(*turn(pair, u))

        def norm1(eng, u):
            eng.wait_ge(s_rs1, u + 1)
            if u >= 2:
                eng.wait_ge(s_kT, u - 1)
            for b in range(UB):
                last = eng.tensor_scalar(kn[:, u % 2, b, :], xt[:, u * UB + b, :], mv1[:, u % 2, b, 0:1],
                                         rs1[:, u % 2, b:b + 1], ALU.subtract, ALU.mult)
            last.then_inc(turn(s_kn, u)[0], 1)

        def weigh(eng, u):
            eng.wait_ge(s_ek, u + 1)
            if u % GU == 0:
                eng.wait_ge(s_vc[u // GU], 16)
            if u >= 2:
                eng.wait_ge(s_num, u - 1)
            eng.tensor_tensor(seqs(pk[:, u % 2, :, 1:PITCH]), seqs(ek[:, u % 2, :, 1:PITCH]), unit_view(vc, u),
                              ALU.mult).then_inc(turn(s_pk, u)[0], 1)

        def divide(eng, u):
            eng.wait_ge(s_num, u + 1)
            eng.wait_ge(s_rd, u + 1)
            if u >= 2:
                wait_turn(eng, s_x1, u - 2)
            eng.tensor_tensor(yk[:, u % 2, :, :], num[:, u % 2, :, :], rden[:, u % 2, :, :],
                              ALU.mult).then_inc(turn(s_yk, u)[0], 1)

        def add_y(eng, u):
            if u % GU == 0:
                eng.wait_ge(s_xc[u // GU], 16)
            wait_turn(eng, s_yk, u)
            eng.tensor_tensor(unit_view(xc, u), unit_view(xc, u), seqs(yk[:, u % 2, :, :]),
                              ALU.add).then_inc(turn(s_x1, u)[0], 1)

        @block.gpsimd
        def _(pool):
            nc.gpsimd.memset(mhalf[:, :], -0.5).then_inc(s_const, 1)
            nc.gpsimd.memset(ident[:, :], 0.0).then_inc(s_const, 1)
            pool.wait_ge(s_const, 2)
            nc.gpsimd.affine_select(out=ident[:, :], in_=ident[:, :], compare_op=ALU.not_equal, fill=1.0,
                                    base=0, pattern=[[-1, P]], channel_multiplier=1).then_inc(s_ident, 1)

            def rstd1(u):
                pool.wait_ge(s_ve1, u + 1)
                if u >= 2:
                    wait_turn(pool, s_kn, u - 2)
                nc.gpsimd.tensor_tensor(rs1[:, u % 2, :], ve1[:, u % 2, :], mhalf[:, :], ALU.pow).then_inc(s_rs1, 1)

            def rstd2(u):
                pool.wait_ge(s_ve2, u + 1)
                if u >= 1:
                    pool.wait_ge(s_nt, u)
                nc.gpsimd.tensor_tensor(rs2[:, :], ve2[:, :], mhalf[:, :], ALU.pow).then_inc(s_rs2, 1)

            def low_h(n):
                g, m = divmod(n, MC)
                pool.wait_ge(s_hh, n + 1)
                if g >= 1:
                    pool.wait_ge(s_dn, n - MC + 1)
                nc.gpsimd.tensor_tensor(hl[:, m, :], h[:, n % HS, :], hh[:, m, :].bitcast(F32),
                                        ALU.subtract).then_inc(s_hl, 1)

            def weights_low(i):
                k, o, size = PIECES[i]
                pool.wait_ge(s_whi, k + 1)
                raw, hi, lo = w_flat[k]
                nc.gpsimd.tensor_tensor(lo[:, o:o + size], raw[:, o:o + size], hi[:, o:o + size].bitcast(F32),
                                        ALU.subtract).then_inc(s_wlo, 1)

            rstd1(0); rstd1(1); weights_low(0); weights_low(1); rstd1(2); weights_low(2); norm1(pool, 2)
            weights_low(3); rstd2(0); rstd1(3); weigh(pool, 2); norm1(pool, 3); weights_low(4); rstd1(4)
            weights_low(5); weigh(pool, 3); weights_low(6); norm1(pool, 4); rstd2(1); rstd1(5); divide(pool, 2)
            norm1(pool, 5); add_y(pool, 2); weigh(pool, 4); rstd2(2); divide(pool, 3); weigh(pool, 5); rstd1(6)
            add_y(pool, 3); rstd1(7); norm1(pool, 6)
            low_h(0)
            low_h(1); norm1(pool, 7); rstd2(3)
            low_h(2); divide(pool, 4); add_y(pool, 4)
            low_h(3); weigh(pool, 6)
            low_h(4); rstd2(4); divide(pool, 5)
            low_h(6); add_y(pool, 5)
            low_h(7); weigh(pool, 7); rstd2(5); divide(pool, 6); add_y(pool, 6)
            low_h(8)
            low_h(9); rstd2(6); divide(pool, 7)
            low_h(10); add_y(pool, 7); rstd2(7)
            low_h(12)
            low_h(13)
            low_h(14)
            low_h(15)
            low_h(16)
            low_h(18)
            low_h(19)
            low_h(20)
            low_h(21)
            low_h(22)

        @block.scalar
        def _(act):
            def tables(name):
                nc.scalar.preload_act_table_set(name)

            tables(LN_EXP)
            act.wait_ge(s_vec, 16)
            nc.scalar.activation(edc[:, :], vec[:, V_TD:V_TD + CC], ACT.Exp).then_inc(s_edc, 1)
            act.wait_ge(s_edc, 1)
            nc.scalar.activation(dcol[:, :], edc[:, :], ACT.Exp, scale=-1.0).then_inc(s_dcol, 1)
            act.wait_ge(s_tfc, 2)
            nc.scalar.activation(fcol[:, :], tfc[:, :], ACT.Exp).then_inc(s_f, 1)

            def expk(u):
                act.wait_ge(s_kT, u + 1)
                if u >= 2:
                    act.wait_ge(s_num, u - 1)
                for c in range(CC):
                    last = nc.scalar.activation(ek[:, u % 2, c * UB:(c + 1) * UB, 1:PITCH], ps_k[:, c, :, :],
                                                ACT.Exp, bias=nsc[:, c:c + 1])
                last.then_inc(s_ek, 1)

            def log_den(u):
                act.wait_ge(s_den, u + 1)
                if u >= 2:
                    act.wait_ge(s_rd, u - 1)
                nc.scalar.activation(lden[:, u % 2, :, :], den[:, u % 2, :, :], ACT.Ln).then_inc(s_ln, 1)

            def recip(u):
                act.wait_ge(s_ln, u + 1)
                if u >= 2:
                    wait_turn(act, s_yk, u - 2)
                nc.scalar.activation(rden[:, u % 2, :, :], lden[:, u % 2, :, :], ACT.Exp, scale=-1.0).then_inc(s_rd, 1)

            def norm2(u):
                act.wait_ge(s_nb2, u + 1)
                if u >= 1:
                    act.wait_ge(s_nT, u)
                for b in range(UB):
                    last = nc.scalar.activation(nt[:, b, :], ps_x[:, b * C:(b + 1) * C], ACT.Identity,
                                                scale=rs2[:, b:b + 1], bias=nb2[:, b:b + 1])
                last.then_inc(s_nt, 1)

            def high_n(u):
                g = u // GU
                act.wait_ge(s_nT, u + 1)
                if g >= 2:
                    act.wait_ge(s_gu, MC * (g - 1))
                o = (u % GU) * UT
                nc.scalar.activation(xh[:, g % 2, :, o:o + UT], ps_x[:, :].rearrange("p (c n) -> p c n", c=CC),
                                     ACT.Copy).then_inc(s_xh, 1)

            def silu(n):
                g, m = divmod(n, MC)
                act.wait_ge(s_gu, n + 1)
                if n >= 2:
                    act.wait_ge(s_h, n - 1)
                if m < FULL:
                    nc.scalar.activation(sil[:, m % 2, :], ps_f[:, m % 2, 0, :], ACT.Silu,
                                         scale=vec[:, V_GS + m:V_GS + m + 1]).then_inc(s_sil, 1)
                else:
                    nc.scalar.activation(sil[REST:P, m % 2, :], ps_f[0:REST, m % 2, 0, :], ACT.Silu,
                                         scale=vec[0:REST, V_GS + m:V_GS + m + 1]).then_inc(s_sil, 1)

            def high_h(n):
                g, m = divmod(n, MC)
                act.wait_ge(s_h, n + 1)
                if g >= 1:
                    act.wait_ge(s_dn, n - MC + 1)
                if m < FULL:
                    nc.scalar.activation(hh[:, m, :], h[:, n % HS, :], ACT.Copy).then_inc(s_hh, 1)
                else:
                    nc.scalar.activation(hx[REST:P, :], h[REST:P, n % HS, :], ACT.Copy).then_inc(s_hh, 1)

            def weights_high(k):
                act.wait_ge((s_wgu, s_wd)[k], 16)
                raw, hi, lo = w_flat[k]
                nc.scalar.activation(hi, raw, ACT.Copy).then_inc(s_whi, 1)

            def weights_sum(k):
                act.wait_ge(s_wlo, PIECES_OF[0] if k == 0 else len(PIECES))
                raw, hi, lo = w_flat[k]
                nc.scalar.activation(junk[:, 0:lo.shape[1]], lo.bitcast(F32), ACT.Abs,
                                     accum_out=wsum[:, k:k + 1]).then_inc(s_wsum, 1)

            expk(0); weights_high(0); log_den(0); recip(0); expk(1); weights_high(1); expk(2); log_den(1)
            recip(1); norm2(0); expk(3); high_n(0); weights_sum(0); log_den(2); recip(2); weights_sum(1)
            norm2(1); expk(4); high_n(1); log_den(3); recip(3); expk(5)
            tables(SILU)
            silu(0); norm2(2)
            silu(1); high_h(0)
            silu(2); high_h(1); high_n(2)
            silu(3); high_h(2)
            silu(4)
            tables(LN_EXP); log_den(4); high_h(3); recip(4); norm2(3); expk(6); high_n(3); log_den(5); recip(5)
            tables(SILU)
            silu(5)
            silu(6); high_h(4); high_h(5)
            silu(7); high_h(6); norm2(4); high_h(7)
            silu(8); high_n(4)
            tables(LN_EXP); expk(7); log_den(6); recip(6)
            tables(SILU)
            silu(9); norm2(5)
            silu(10); high_n(5); high_h(8)
            silu(11)
            tables(LN_EXP); log_den(7); high_h(9); recip(7)
            tables(SILU)
            silu(12); norm2(6); high_h(10)
            silu(13); high_h(11); high_n(6); high_h(12)
            silu(14); high_h(13); norm2(7)
            silu(15); high_n(7)
            silu(16); high_h(14); high_h(15)
            silu(17); high_h(16)
            silu(18); high_h(17); high_h(18)
            silu(19)
            silu(20); high_h(19)
            silu(21); high_h(20)
            silu(22); high_h(21); high_h(22)
            silu(23); high_h(23)

        @block.vector
        def _(dve):
            nc.vector.memset(decay[:, :, :], 0.0).then_inc(s_zero, 1)
            nc.vector.memset(ones[:, :], 1.0).then_inc(s_ones, 1)
            dve.wait_ge(s_vec, 16)
            nc.vector.tensor_scalar(tfc[:, :], vec[:, V_TF:V_TF + CC], F_MAX, None, ALU.min).then_inc(s_tfc, 1)
            dve.wait_ge(s_tfc, 1)
            nc.vector.tensor_scalar(nsc[:, :], tfc[:, :], 0.0, -1.0, ALU.max, ALU.mult).then_inc(s_tfc, 1)

            def decay_tile():
                dve.wait_ge(s_zero, 1)
                dve.wait_ge(s_dcol, 1)
                for c in range(CC):
                    cols = decay[:, c * UB:(c + 1) * UB, 2:PITCH]
                    last = nc.vector.tensor_scalar(cols, cols, dcol[:, c:c + 1], None, ALU.add)
                last.then_inc(s_decay, 1)

            def weights_any():
                dve.wait_ge(s_wsum, 2)
                nc.vector.tensor_scalar(wany[:, :], wsum[:, :], 0.0, None, ALU.is_gt).then_inc(s_wany, 1)

            def publish():
                dve.wait_ge(s_wcnt, 1)
                nc.vector.tensor_copy(flag[:, :], ps_d[0:1, 0, 0:1]).then_inc(s_flag, 1)

            def stats1(u):
                if u % GU == 0:
                    dve.wait_ge(s_xt[u // GU], 16)
                if u >= 2:
                    dve.wait_ge(s_mv1, u - 1)
                for b in range(UB):
                    last = nc.vector.bn_stats(st1[:, u % 2, b, :], xt[:, u * UB + b, :])
                last.then_inc(s_st1, 1)

            def aggr1(u):
                dve.wait_ge(s_st1, u + 1)
                if u >= 2:
                    wait_turn(dve, s_kn, u - 2)
                for b in range(UB):
                    last = nc.vector.bn_aggr(mv1[:, u % 2, b, :], st1[:, u % 2, b, :])
                last.then_inc(s_mv1, 1)

            def eps1(u):
                dve.wait_ge(s_mv1, u + 1)
                if u >= 2:
                    dve.wait_ge(s_rs1, u - 1)
                nc.vector.tensor_scalar(ve1[:, u % 2, :], mv1[:, u % 2, :, 1], EPS, None, ALU.add).then_inc(s_ve1, 1)

            def pads(u):
                s = u % 2
                dve.wait_ge(s_ek, u + 1)
                nc.vector.tensor_copy(ek[:, s, :, 0:1], ek[:, s, :, 1:2]).then_inc(s_pad, 1)
                wait_turn(dve, s_pk, u)
                nc.vector.tensor_copy(pk[:, s, :, 0:1], pk[:, s, :, 1:2]).then_inc(s_pad, 1)

            def scan(u):
                s = u % 2
                if u == 0:
                    dve.wait_ge(s_decay, 1)
                if u >= 2:
                    dve.wait_ge(s_num, u - 1)
                dve.wait_ge(s_pad, 2 * u + 2)
                flat = [t.rearrange("p q t -> p (q t)") for t in (sbb[:, s, :, :], sa[:, s, :, :], decay[:, :, :],
                                                                  ek[:, s, :, :], pk[:, s, :, :])]
                nc.vector.tensor_tensor_scan(flat[0], flat[2], flat[3], 0.0, ALU.mult, ALU.add).then_inc(s_sb, 1)
                nc.vector.tensor_tensor_scan(flat[1], flat[2], flat[4], 0.0, ALU.mult, ALU.add).then_inc(s_sa, 1)

            def denom(u):
                s = u % 2
                if u == 0:
                    dve.wait_ge(s_f, 1)
                if u >= 2:
                    dve.wait_ge(s_ln, u - 1)
                dve.wait_ge(s_sb, u + 1)
                for c in range(CC):
                    q = slice(c * UB, (c + 1) * UB)
                    last = nc.vector.scalar_tensor_tensor(den[:, s, q, :], ek[:, s, q, 1:PITCH], fcol[:, c:c + 1],
                                                          sbb[:, s, q, 0:T], ALU.mult, ALU.add)
                last.then_inc(s_den, 1)

            def numer(u):
                s = u % 2
                if u >= 2:
                    wait_turn(dve, s_yk, u - 2)
                dve.wait_ge(s_sa, u + 1)
                for c in range(CC):
                    q = slice(c * UB, (c + 1) * UB)
                    last = nc.vector.scalar_tensor_tensor(num[:, s, q, :], pk[:, s, q, 1:PITCH], fcol[:, c:c + 1],
                                                          sa[:, s, q, 0:T], ALU.mult, ALU.add)
                last.then_inc(s_num, 1)

            def stats2(u):
                dve.wait_ge(s_x1T, u + 1)
                if u >= 1:
                    dve.wait_ge(s_mv2, u)
                for b in range(UB):
                    last = nc.vector.bn_stats(st2[:, b, :], ps_x[:, b * C:(b + 1) * C])
                last.then_inc(s_st2, 1)

            def aggr2(u):
                dve.wait_ge(s_st2, u + 1)
                if u >= 1:
                    dve.wait_ge(s_nb2, u)
                for b in range(UB):
                    last = nc.vector.bn_aggr(mv2[:, b, :], st2[:, b, :])
                last.then_inc(s_mv2, 1)

            def eps2(u):
                dve.wait_ge(s_mv2, u + 1)
                if u >= 1:
                    dve.wait_ge(s_rs2, u)
                nc.vector.tensor_scalar(ve2[:, :], mv2[:, :, 1], EPS, None, ALU.add).then_inc(s_ve2, 1)

            def bias2(u):
                dve.wait_ge(s_rs2, u + 1)
                if u >= 1:
                    dve.wait_ge(s_nt, u)
                nc.vector.scalar_tensor_tensor(nb2[:, :], mv2[:, :, 0], -1.0, rs2[:, :], ALU.mult,
                                               ALU.mult).then_inc(s_nb2, 1)

            def low_n(u):
                g = u // GU
                dve.wait_ge(s_xh, u + 1)
                if g >= 2:
                    dve.wait_ge(s_gu, MC * (g - 1))
                o = (u % GU) * UT
                nc.vector.tensor_tensor(xl[:, g % 2, :, o:o + UT], ps_x[:, :].rearrange("p (c n) -> p c n", c=CC),
                                        xh[:, g % 2, :, o:o + UT].bitcast(F32), ALU.subtract).then_inc(s_xl, 1)

            def gated(n):
                g, m = divmod(n, MC)
                dve.wait_ge(s_sil, n + 1)
                if n >= HS:
                    dve.wait_ge(s_hh, n - HS + 1)
                    wait_low(dve, n - HS)
                r = slice(0, P) if m < FULL else slice(REST, P)
                part = 1 if m < FULL else 0
                nc.vector.scalar_tensor_tensor(h[r, n % HS, :], ps_f[r, m % 2, part, :], vec[r, V_US + m:V_US + m + 1],
                                               sil[r, m % 2, :], ALU.mult, ALU.mult).then_inc(s_h, 1)

            def low_rest(n):
                dve.wait_ge(s_hh, n + 1)
                if n >= MC:
                    dve.wait_ge(s_dn, n - MC + 1)
                nc.vector.tensor_tensor(hx[0:REST, :], h[REST:P, n % HS, :], hx[REST:P, :].bitcast(F32),
                                        ALU.subtract).then_inc(s_hx, 1)

            def finish(g):
                dve.wait_ge(s_dn, MC * (g + 1))
                wait_turn(dve, s_x1, GU * (g + 1) - 1)
                ts = slice(g * GT, (g + 1) * GT)
                for c in range(CC):
                    nc.vector.scalar_tensor_tensor(xc[:, c, ts], ps_d[:, c, :], vec[:, V_DS + c:V_DS + c + 1],
                                                   xc[:, c, ts], ALU.mult, ALU.add).then_inc(s_fin, 1)

            stats1(0); stats1(1); aggr1(0); eps1(0); norm1(dve, 0); aggr1(1); weigh(dve, 0); eps1(1)
            decay_tile(); pads(0); scan(0); norm1(dve, 1); denom(0); numer(0); stats1(2); aggr1(2); stats1(3)
            divide(dve, 0); eps1(2); weigh(dve, 1); add_y(dve, 0); aggr1(3); pads(1); stats2(0); eps1(3)
            aggr2(0); scan(1); stats1(4); eps2(0); aggr1(4); denom(1); stats1(5); numer(1); bias2(0)
            divide(dve, 1); pads(2); eps1(4); scan(2); denom(2); low_n(0); add_y(dve, 1); numer(2); stats2(1)
            aggr2(1); aggr1(5); eps1(5); eps2(1); pads(3); scan(3); bias2(1); weights_any(); denom(3); publish()
            stats1(6); aggr1(6); low_n(1); numer(3); stats2(2); aggr2(2); eps1(6); eps2(2); stats1(7); pads(4)
            bias2(2); aggr1(7)
            gated(0); eps1(7); scan(4)
            gated(1)
            gated(2); denom(4); pads(5); numer(4); low_n(2)
            gated(3); stats2(3); aggr2(3); eps2(3); scan(5); bias2(3); denom(5); numer(5)
            gated(4); low_n(3)
            gated(5); stats2(4); aggr2(4); eps2(4); pads(6)
            gated(6); scan(6); bias2(4)
            gated(7); denom(6); low_rest(5)
            gated(8); low_n(4); numer(6); stats2(5); aggr2(5); eps2(5); finish(0); bias2(5); pads(7)
            gated(9); scan(7)
            gated(10); low_n(5); denom(7); stats2(6)
            gated(11); numer(7); aggr2(6); eps2(6); bias2(6)
            gated(12); low_rest(11); low_n(6)
            gated(13); stats2(7); aggr2(7); eps2(7)
            gated(14); bias2(7); finish(1)
            gated(15); low_n(7)
            gated(16)
            gated(17); low_rest(17)
            gated(18)
            gated(19)
            gated(20); finish(2)
            gated(21)
            gated(22)
            gated(23); low_rest(23); finish(3)

        @block.tensor
        def _(pe):
            def k_T(u):
                wait_turn(pe, s_kn, u)
                if u == 0:
                    pe.wait_ge(s_ident, 1)
                else:
                    pe.wait_ge(s_ek, u)
                for b in range(UB):
                    for c in range(CC):
                        last = nc.tensor.transpose(ps_k[:, c, b, :], kn[:, u % 2, b, c * P:(c + 1) * P], ident[:, :])
                last.then_inc(s_kT, 1)

            def x1_T(u):
                wait_turn(pe, s_x1, u)
                if u >= 1:
                    pe.wait_ge(s_xl, u)
                for b in range(UB):
                    for c in range(CC):
                        t0 = u * UT + b * T
                        last = nc.tensor.transpose(ps_x[:, b * C + c * P:b * C + (c + 1) * P], xc[:, c, t0:t0 + T],
                                                   ident[:, :])
                last.then_inc(s_x1T, 1)

            def n_T(u):
                pe.wait_ge(s_nt, u + 1)
                for b in range(UB):
                    for c in range(CC):
                        last = nc.tensor.transpose(ps_x[:, c * UT + b * T:c * UT + (b + 1) * T],
                                                   nt[:, b, c * P:(c + 1) * P], ident[:, :])
                last.then_inc(s_nT, 1)

            def gate_up(n, weights):
                g, m = divmod(n, MC)
                if m == 0:
                    pe.wait_ge(s_xl, GU * (g + 1))
                if n >= 2:
                    pe.wait_ge(s_h, n - 1)
                for part, tile in (((0, m), (1, FULL + m)) if m < FULL else ((0, 2 * FULL),)):
                    todo = [(w, c, x) for w in weights for c in range(CC) for x in (xh, xl)]
                    for i, (w, c, x) in enumerate(todo):
                        last = nc.tensor.matmul(ps_f[:, m % 2, part, :], w[0][:, c, tile, :], x[:, g % 2, c, :],
                                                start=i == 0, stop=i == len(todo) - 1)
                last.then_inc(s_gu, 1)

            def down(n, weights):
                g, m = divmod(n, MC)
                if m == 0 and g >= 1:
                    pe.wait_ge(s_fin, CC * g)
                wait_low(pe, n)
                for c in range(CC):
                    todo = [(w, a) for w in weights for a in ((hh[:, m, :], hl[:, m, :]) if m < FULL else (hx[:, :],))]
                    for i, (w, a) in enumerate(todo):
                        last = nc.tensor.matmul(ps_d[:, c, :], w[1][:, m, c * P:(c + 1) * P], a,
                                                start=m == 0 and i == 0, stop=m == MC - 1 and i == len(todo) - 1)
                last.then_inc(s_dn, 1)

            def count():
                pe.wait_ge(s_ones, 1)
                pe.wait_ge(s_wany, 1)
                nc.tensor.matmul(ps_d[0:1, 0, 0:1], ones[:, :], wany[:, 0:1], start=True, stop=False)
                nc.tensor.matmul(ps_d[0:1, 0, 0:1], ones[:, :], wany[:, 1:2], start=False, stop=True).then_inc(s_wcnt, 1)

            def feed_forward(weights):
                gate_up(0, weights)
                gate_up(1, weights)
                gate_up(2, weights); n_T(2)
                gate_up(3, weights)
                gate_up(4, weights); x1_T(3); down(0, weights)
                gate_up(5, weights); down(1, weights); k_T(6); n_T(3); k_T(7)
                gate_up(6, weights); x1_T(4); down(2, weights)
                gate_up(7, weights); down(3, weights)
                gate_up(8, weights); n_T(4); down(4, weights)
                gate_up(9, weights); x1_T(5); down(5, weights)
                gate_up(10, weights); down(6, weights); n_T(5)
                gate_up(11, weights); down(7, weights); x1_T(6)
                gate_up(12, weights); down(8, weights)
                gate_up(13, weights); down(9, weights); n_T(6)
                gate_up(14, weights); down(10, weights); x1_T(7)
                gate_up(15, weights); down(11, weights)
                gate_up(16, weights); n_T(7); down(12, weights)
                gate_up(17, weights); down(13, weights)
                gate_up(18, weights); down(14, weights)
                gate_up(19, weights); down(15, weights)
                gate_up(20, weights); down(16, weights)
                gate_up(21, weights); down(17, weights)
                gate_up(22, weights); down(18, weights)
                gate_up(23, weights); down(19, weights); down(20, weights); down(21, weights); down(22, weights)
                down(23, weights)

            k_T(0); k_T(1); x1_T(0); k_T(2); k_T(3); n_T(0); x1_T(1); k_T(4); count(); n_T(1); k_T(5); x1_T(2)
            pe.wait_ge(s_whi, 2)
            pe.wait_ge(s_wlo, len(PIECES))
            pe.wait_ge(s_flag, 1)
            found = pe.value_load(flag[0:1, 0:1], min_val=0, max_val=2 * P)
            with pe.If(found > 0):
                feed_forward([(wgu_hi, wd_hi), (wgu_lo, wd_lo)])
            with pe.Else():
                feed_forward([(wgu_hi, wd_hi)])
            pe.nop()


def kernel(x, ctx_2048, L0_xattn_time_decay, L0_xattn_time_first, L0_ffn_gate_w, L0_ffn_up_w, L0_ffn_down_w,
           L0_ffn_gate_s, L0_ffn_up_s, L0_ffn_down_s):
    import numpy as np
    import concourse.bacc as bacc
    from concourse.bass_utils import run_bass_kernel_spmd

    x, v = np.asarray(x), np.asarray(ctx_2048)
    cut = FULL * P

    def tiles(w, n):
        return w.reshape(n, P, -1).transpose(1, 0, 2)

    gT, uT = np.asarray(L0_ffn_gate_w).T, np.asarray(L0_ffn_up_w).T
    gu = np.concatenate([gT[:, :cut], uT[:, :cut], gT[:, cut:], uT[:, cut:]], axis=1)
    dT = np.asarray(L0_ffn_down_w).T
    dT = np.concatenate([dT[:cut], dT[cut:], dT[cut:]], axis=0)
    gs, us = np.asarray(L0_ffn_gate_s), np.asarray(L0_ffn_up_s)
    cols = [np.asarray(L0_xattn_time_decay), np.asarray(L0_xattn_time_first), np.concatenate([gs, gs[cut:]]),
            np.concatenate([us, us[cut:]]), np.asarray(L0_ffn_down_s)]
    arrays = {
        "x_tok": x,
        "x_ch": x.reshape(B * T, C).T,
        "v_ch": v.reshape(B * T, C).T,
        "w_gu": tiles(gu, CC).reshape(P, CC * GUC * P),
        "w_d": tiles(dT, MC).reshape(P, MC * C),
        "vecs": np.concatenate([a.reshape(-1, P) for a in cols], axis=0).T,
    }
    arrays = {k: np.ascontiguousarray(a) for k, a in arrays.items()}
    nc = bacc.Bacc("TRN2", target_bir_lowering=False, num_devices=1)
    args = [nc.dram_tensor(k, a.shape, F32, kind="ExternalInput").ap() for k, a in arrays.items()]
    out = nc.dram_tensor("out_ch", (C, B * T), F32, kind="ExternalOutput").ap()
    build(nc, *args, out)
    r = run_bass_kernel_spmd(nc, [arrays], core_ids=[0])
    return np.ascontiguousarray(r.results[0]["out_ch"].T).reshape(B, T, C)
```

```python
from contextlib import ExitStack

import concourse.bass as bass
from concourse import mybir

ALU = mybir.AluOpType
ACT = mybir.ActivationFunctionType
F32 = mybir.dt.float32
F32R = mybir.dt.float32r
I32 = mybir.dt.int32
AX_X = mybir.AxisListType.X

P = 128
B, T, C = 16, 128, 256
INTER = 704
CC = C // P
UB = 2
UT = UB * T
UNITS = B // UB
GU = 2
GT = GU * UT
GROUPS = UNITS // GU
SEG = CC * UB
PITCH = T + 1
FULL = INTER // P
REST = INTER - FULL * P
MC = FULL + 1
GUC = 2 * FULL + 1
EPS = 1e-5
F_MAX = 70.0
V_TD, V_TF, V_GS, V_US, V_DS = 0, CC, 2 * CC, 2 * CC + MC, 2 * CC + 2 * MC
V_N = V_DS + CC
EARLY = 2
HS = 4
LN_EXP, SILU = "natural_log_exp_and_others", "silu_and_others"
W_SIZES = (CC * GUC * P, MC * C)
PIECES_OF = (4, 3)
PIECES = [(k, i * (W_SIZES[k] // n), W_SIZES[k] // n) for k, n in enumerate(PIECES_OF) for i in range(n)]
assert 2 * REST == P and GT == 512


def build(nc, x_tok, x_ch, v_ch, w_gu, w_d, vecs, out_ch):
    with ExitStack() as ctx:
        def sb(name, shape, dt=F32):
            return ctx.enter_context(nc.sbuf_tensor(name, shape, dt))

        def psum(name, shape):
            return ctx.enter_context(nc.psum_tensor(name, shape, F32))

        def sem(name):
            return ctx.enter_context(nc.semaphore(name))

        xt = sb("xt", [P, B, C])
        xc = sb("xc", [P, CC, B * T])
        vc = sb("vc", [P, CC, B * T])
        wgu = sb("wgu", [P, CC * GUC * P])
        wgu_hi = sb("wgu_hi", [P, CC, GUC, P], F32R)
        wgu_lo = sb("wgu_lo", [P, CC, GUC, P], F32R)
        wd = sb("wd", [P, MC * C])
        wd_hi = sb("wd_hi", [P, MC, C], F32R)
        wd_lo = sb("wd_lo", [P, MC, C], F32R)
        vec = sb("vec", [P, V_N])
        ident = sb("ident", [P, P])
        ones = sb("ones", [P, 1])
        mhalf = sb("mhalf", [P, UB])
        decay = sb("decay", [P, SEG, PITCH])
        edc = sb("edc", [P, CC])
        dcol = sb("dcol", [P, CC])
        tfc = sb("tfc", [P, CC])
        nsc = sb("nsc", [P, CC])
        fcol = sb("fcol", [P, CC])
        wsum = sb("wsum", [P, 2])
        wany = sb("wany", [P, 2])
        flag = sb("flag", [1, 1], I32)
        st1 = sb("st1", [P, 2, UB, 6])
        mv1 = sb("mv1", [P, 2, UB, 2])
        ve1 = sb("ve1", [P, 2, UB])
        rs1 = sb("rs1", [P, 2, UB])
        kn = sb("kn", [P, 2, UB, C])
        ek = sb("ek", [P, 2, SEG, PITCH])
        pk = sb("pk", [P, 2, SEG, PITCH])
        sa = sb("sa", [P, 2, SEG, PITCH])
        sbb = sb("sbb", [P, 2, SEG, PITCH])
        num = sb("num", [P, 2, SEG, T])
        den = sb("den", [P, 2, SEG, T])
        lden = sb("lden", [P, 2, SEG, T])
        rden = sb("rden", [P, 2, SEG, T])
        yk = sb("yk", [P, 2, SEG, T])
        st2 = sb("st2", [P, UB, 6])
        mv2 = sb("mv2", [P, UB, 2])
        ve2 = sb("ve2", [P, UB])
        rs2 = sb("rs2", [P, UB])
        nb2 = sb("nb2", [P, UB])
        nt = sb("nt", [P, UB, C])
        xh = sb("xh", [P, 2, CC, GT], F32R)
        xl = sb("xl", [P, 2, CC, GT], F32R)
        sil = sb("sil", [P, 2, GT])
        h = sb("h", [P, HS, GT])
        hh = sb("hh", [P, FULL, GT], F32R)
        hl = sb("hl", [P, FULL, GT], F32R)
        hx = sb("hx", [P, GT], F32R)

        ps_k = psum("ps_k", [P, CC, UB, T])
        ps_x = psum("ps_x", [P, 512])
        ps_f = psum("ps_f", [P, 2, 2, GT])
        ps_d = psum("ps_d", [P, CC, GT])

        s_vec = sem("s_vec")
        s_xt = [sem(f"s_xt{u}") for u in range(UNITS)]
        s_xc = [sem(f"s_xc{g}") for g in range(GROUPS)]
        s_vc = [sem(f"s_vc{g}") for g in range(GROUPS)]
        s_wgu, s_wd = sem("s_wgu"), sem("s_wd")
        s_out = sem("s_out")
        s_const = sem("s_const")
        s_ident = sem("s_ident")
        s_ones = sem("s_ones")
        s_zero = sem("s_zero")
        s_edc, s_dcol, s_tfc, s_f = sem("s_edc"), sem("s_dcol"), sem("s_tfc"), sem("s_f")
        s_decay = sem("s_decay")
        s_whi = sem("s_whi")
        s_wsum = sem("s_wsum")
        s_wany, s_wcnt, s_flag = (sem(n) for n in ("s_wany", "s_wcnt", "s_flag"))
        s_wlo = sem("s_wlo")
        s_st1, s_mv1, s_ve1, s_rs1 = (sem(n) for n in ("s_st1", "s_mv1", "s_ve1", "s_rs1"))
        s_kT, s_ek, s_pad = (sem(n) for n in ("s_kT", "s_ek", "s_pad"))
        s_kn, s_pk, s_yk, s_x1 = ((sem(n + "_early"), sem(n)) for n in ("s_kn", "s_pk", "s_yk", "s_x1"))
        s_sb, s_sa, s_den, s_num, s_ln, s_rd = (sem(n) for n in ("s_sb", "s_sa", "s_den", "s_num", "s_ln", "s_rd"))
        s_x1T, s_st2, s_mv2, s_ve2, s_rs2, s_nb2, s_nt, s_nT, s_xh, s_xl = (sem(n) for n in (
            "s_x1T", "s_st2", "s_mv2", "s_ve2", "s_rs2", "s_nb2", "s_nt", "s_nT", "s_xh", "s_xl"))
        s_gu, s_sil, s_h, s_hh, s_hl, s_dn = (sem(n) for n in ("s_gu", "s_sil", "s_h", "s_hh", "s_hl", "s_dn"))
        s_hx = sem("s_hx")
        s_fin = sem("s_fin")

        def unit_cols(u):
            return slice(u * UT, (u + 1) * UT)

        def unit_view(t, u):
            return t[:, :, unit_cols(u)].rearrange("p c (b t) -> p c b t", t=T)

        def seqs(t):
            return t.rearrange("p (c b) t -> p c b t", c=CC)

        w_flat = [(wgu[:, :], wgu_hi[:, :, :, :].rearrange("p c m n -> p (c m n)"),
                   wgu_lo[:, :, :, :].rearrange("p c m n -> p (c m n)")),
                  (wd[:, :], wd_hi[:, :, :].rearrange("p m n -> p (m n)"),
                   wd_lo[:, :, :].rearrange("p m n -> p (m n)"))]

        def wait_low(eng, n):
            g, m = divmod(n, MC)
            if m < FULL:
                eng.wait_ge(s_hl, FULL * g + m + 1)
            else:
                eng.wait_ge(s_hx, g + 1)

        block = ctx.enter_context(nc.Block())

        @block.sync
        def _(sp):
            def load_group(g):
                ts = slice(g * GT, (g + 1) * GT)
                for u in range(g * GU, (g + 1) * GU):
                    bs = slice(u * UB, (u + 1) * UB)
                    sp.dma_start(xt[:, bs, :], x_tok[bs, :, :].rearrange("b t c -> t b c")).then_inc(s_xt[u], 16)
                sp.dma_start(vc[:, :, ts], v_ch[:, ts].rearrange("(k p) n -> p k n", p=P)).then_inc(s_vc[g], 16)
                sp.dma_start(xc[:, :, ts], x_ch[:, ts].rearrange("(k p) n -> p k n", p=P)).then_inc(s_xc[g], 16)

            load_group(0)
            sp.dma_start(wgu[:, :], w_gu).then_inc(s_wgu, 16)
            sp.dma_start(wd[:, :], w_d).then_inc(s_wd, 16)
            for g in range(1, GROUPS):
                load_group(g)
            for g in range(GROUPS):
                for c in range(CC):
                    sp.wait_ge(s_fin, CC * g + c + 1)
                    sp.dma_start(out_ch[c * P:(c + 1) * P, g * GT:(g + 1) * GT],
                                 xc[:, c, g * GT:(g + 1) * GT]).then_inc(s_out, 16)
            sp.wait_ge(s_out, 16 * GROUPS * CC)

        def turn(pair, u):
            return (pair[0], u + 1) if u < EARLY else (pair[1], u - EARLY + 1)

        def wait_turn(eng, pair, u):
            eng.wait_ge(*turn(pair, u))

        def norm1(eng, u):
            eng.wait_ge(s_rs1, u + 1)
            if u >= 2:
                eng.wait_ge(s_kT, u - 1)
            for b in range(UB):
                last = eng.tensor_scalar(kn[:, u % 2, b, :], xt[:, u * UB + b, :], mv1[:, u % 2, b, 0:1],
                                         rs1[:, u % 2, b:b + 1], ALU.subtract, ALU.mult)
            last.then_inc(turn(s_kn, u)[0], 1)

        def weigh(eng, u):
            eng.wait_ge(s_ek, u + 1)
            if u % GU == 0:
                eng.wait_ge(s_vc[u // GU], 16)
            if u >= 2:
                eng.wait_ge(s_num, u - 1)
            eng.tensor_tensor(seqs(pk[:, u % 2, :, 1:PITCH]), seqs(ek[:, u % 2, :, 1:PITCH]), unit_view(vc, u),
                              ALU.mult).then_inc(turn(s_pk, u)[0], 1)

        def divide(eng, u):
            eng.wait_ge(s_num, u + 1)
            eng.wait_ge(s_rd, u + 1)
            if u >= 2:
                wait_turn(eng, s_x1, u - 2)
            eng.tensor_tensor(yk[:, u % 2, :, :], num[:, u % 2, :, :], rden[:, u % 2, :, :],
                              ALU.mult).then_inc(turn(s_yk, u)[0], 1)

        def add_y(eng, u):
            if u % GU == 0:
                eng.wait_ge(s_xc[u // GU], 16)
            wait_turn(eng, s_yk, u)
            eng.tensor_tensor(unit_view(xc, u), unit_view(xc, u), seqs(yk[:, u % 2, :, :]),
                              ALU.add).then_inc(turn(s_x1, u)[0], 1)

        @block.gpsimd
        def _(pool):
            nc.gpsimd.memset(mhalf[:, :], -0.5).then_inc(s_const, 1)
            nc.gpsimd.memset(ident[:, :], 0.0).then_inc(s_const, 1)
            pool.wait_ge(s_const, 2)
            nc.gpsimd.affine_select(out=ident[:, :], in_=ident[:, :], compare_op=ALU.not_equal, fill=1.0,
                                    base=0, pattern=[[-1, P]], channel_multiplier=1).then_inc(s_ident, 1)

            def rstd1(u):
                pool.wait_ge(s_ve1, u + 1)
                if u >= 2:
                    wait_turn(pool, s_kn, u - 2)
                nc.gpsimd.tensor_tensor(rs1[:, u % 2, :], ve1[:, u % 2, :], mhalf[:, :], ALU.pow).then_inc(s_rs1, 1)

            def rstd2(u):
                pool.wait_ge(s_ve2, u + 1)
                if u >= 1:
                    pool.wait_ge(s_nt, u)
                nc.gpsimd.tensor_tensor(rs2[:, :], ve2[:, :], mhalf[:, :], ALU.pow).then_inc(s_rs2, 1)

            def low_h(n):
                g, m = divmod(n, MC)
                pool.wait_ge(s_hh, n + 1)
                if g >= 1:
                    pool.wait_ge(s_dn, CC * (n - MC + 1))
                nc.gpsimd.tensor_tensor(hl[:, m, :], h[:, n % HS, :], hh[:, m, :].bitcast(F32),
                                        ALU.subtract).then_inc(s_hl, 1)

            def weights_low(i):
                k, o, size = PIECES[i]
                pool.wait_ge(s_whi, k + 1)
                raw, hi, lo = w_flat[k]
                nc.gpsimd.tensor_tensor(lo[:, o:o + size], raw[:, o:o + size], hi[:, o:o + size].bitcast(F32),
                                        ALU.subtract).then_inc(s_wlo, 1)

            rstd1(0); rstd1(1); weights_low(0); weights_low(1); rstd1(2); weights_low(2); rstd1(3); rstd2(0)
            weights_low(3); weigh(pool, 2); weights_low(4); rstd1(4); weights_low(5); weights_low(6)
            weigh(pool, 3); rstd2(1); divide(pool, 2); add_y(pool, 2); weigh(pool, 4); rstd1(5); divide(pool, 3)
            rstd2(2)
            low_h(0); add_y(pool, 3)
            low_h(1); rstd1(6); weigh(pool, 5); rstd2(3); divide(pool, 4)
            low_h(2); add_y(pool, 4); rstd1(7)
            low_h(3); weigh(pool, 6); rstd2(4)
            low_h(4); divide(pool, 5); add_y(pool, 5)
            low_h(6)
            low_h(7); weigh(pool, 7); rstd2(5); divide(pool, 6)
            low_h(8); add_y(pool, 6)
            low_h(9)
            low_h(10); rstd2(6); divide(pool, 7); add_y(pool, 7)
            low_h(12); rstd2(7)
            low_h(13)
            low_h(14)
            low_h(15)
            low_h(16)
            low_h(18)
            low_h(19)
            low_h(20)
            low_h(21)
            low_h(22)

        @block.scalar
        def _(act):
            def tables(name):
                nc.scalar.preload_act_table_set(name)

            act.dma_start(vec[:, :], vecs).then_inc(s_vec, 16)
            tables(LN_EXP)
            act.wait_ge(s_vec, 16)
            nc.scalar.activation(edc[:, :], vec[:, V_TD:V_TD + CC], ACT.Exp).then_inc(s_edc, 1)
            act.wait_ge(s_edc, 1)
            nc.scalar.activation(dcol[:, :], edc[:, :], ACT.Exp, scale=-1.0).then_inc(s_dcol, 1)
            act.wait_ge(s_tfc, 2)
            nc.scalar.activation(fcol[:, :], tfc[:, :], ACT.Exp).then_inc(s_f, 1)

            def expk(u):
                act.wait_ge(s_kT, u + 1)
                if u >= 2:
                    act.wait_ge(s_num, u - 1)
                for c in range(CC):
                    last = nc.scalar.activation(ek[:, u % 2, c * UB:(c + 1) * UB, 1:PITCH], ps_k[:, c, :, :],
                                                ACT.Exp, bias=nsc[:, c:c + 1])
                last.then_inc(s_ek, 1)

            def log_den(u):
                act.wait_ge(s_den, u + 1)
                if u >= 2:
                    act.wait_ge(s_rd, u - 1)
                nc.scalar.activation(lden[:, u % 2, :, :], den[:, u % 2, :, :], ACT.Ln).then_inc(s_ln, 1)

            def recip(u):
                act.wait_ge(s_ln, u + 1)
                if u >= 2:
                    wait_turn(act, s_yk, u - 2)
                nc.scalar.activation(rden[:, u % 2, :, :], lden[:, u % 2, :, :], ACT.Exp, scale=-1.0).then_inc(s_rd, 1)

            def norm2(u):
                act.wait_ge(s_nb2, u + 1)
                if u >= 1:
                    act.wait_ge(s_nT, u)
                for b in range(UB):
                    last = nc.scalar.activation(nt[:, b, :], ps_x[:, b * C:(b + 1) * C], ACT.Identity,
                                                scale=rs2[:, b:b + 1], bias=nb2[:, b:b + 1])
                last.then_inc(s_nt, 1)

            def high_n(u):
                g = u // GU
                act.wait_ge(s_nT, u + 1)
                if g >= 2:
                    act.wait_ge(s_gu, MC * (g - 1))
                o = (u % GU) * UT
                nc.scalar.activation(xh[:, g % 2, :, o:o + UT], ps_x[:, :].rearrange("p (c n) -> p c n", c=CC),
                                     ACT.Copy).then_inc(s_xh, 1)

            def silu(n):
                g, m = divmod(n, MC)
                act.wait_ge(s_gu, n + 1)
                if n >= 2:
                    act.wait_ge(s_h, n - 1)
                if m < FULL:
                    nc.scalar.activation(sil[:, m % 2, :], ps_f[:, m % 2, 0, :], ACT.Silu,
                                         scale=vec[:, V_GS + m:V_GS + m + 1]).then_inc(s_sil, 1)
                else:
                    nc.scalar.activation(sil[REST:P, m % 2, :], ps_f[0:REST, m % 2, 0, :], ACT.Silu,
                                         scale=vec[0:REST, V_GS + m:V_GS + m + 1]).then_inc(s_sil, 1)

            def high_h(n):
                g, m = divmod(n, MC)
                act.wait_ge(s_h, n + 1)
                if g >= 1:
                    act.wait_ge(s_dn, CC * (n - MC + 1))
                if m < FULL:
                    nc.scalar.activation(hh[:, m, :], h[:, n % HS, :], ACT.Copy).then_inc(s_hh, 1)
                else:
                    nc.scalar.activation(hx[REST:P, :], h[REST:P, n % HS, :], ACT.Copy).then_inc(s_hh, 1)

            def weights_high(k):
                act.wait_ge((s_wgu, s_wd)[k], 16)
                raw, hi, lo = w_flat[k]
                nc.scalar.activation(hi, raw, ACT.Copy).then_inc(s_whi, 1)

            def weights_sum(k):
                act.wait_ge(s_wlo, PIECES_OF[0] if k == 0 else len(PIECES))
                raw, hi, lo = w_flat[k]
                nc.scalar.activation(raw, lo.bitcast(F32), ACT.Abs,
                                     accum_out=wsum[:, k:k + 1]).then_inc(s_wsum, 1)

            expk(0); expk(1); weights_high(0); log_den(0); recip(0); log_den(1); recip(1); weights_high(1)
            expk(2); norm2(0); expk(3); high_n(0); weights_sum(0); log_den(2); weights_sum(1); recip(2)
            norm2(1); expk(4); high_n(1); log_den(3); recip(3)
            tables(SILU)
            silu(0)
            silu(1); high_h(0); norm2(2); high_h(1)
            silu(2); high_n(2)
            tables(LN_EXP); log_den(4); expk(5); recip(4)
            tables(SILU)
            silu(3); high_h(2)
            silu(4); norm2(3); high_h(3)
            silu(5); high_n(3)
            tables(LN_EXP); log_den(5); expk(6); recip(5)
            tables(SILU)
            silu(6); high_h(4)
            silu(7); high_h(5); norm2(4); high_h(6)
            silu(8); high_n(4); high_h(7)
            tables(LN_EXP); log_den(6); expk(7); recip(6)
            tables(SILU)
            silu(9); high_h(8); norm2(5)
            silu(10); high_h(9); high_n(5); high_h(10)
            silu(11)
            tables(LN_EXP); log_den(7); recip(7)
            tables(SILU)
            silu(12); norm2(6); high_h(11); high_n(6)
            silu(13); high_h(12); high_h(13)
            silu(14); norm2(7)
            silu(15)
            silu(16); high_n(7); high_h(14); high_h(15); high_h(16)
            silu(17); high_h(17)
            silu(18)
            silu(19); high_h(18)
            silu(20); high_h(19); high_h(20)
            silu(21)
            silu(22); high_h(21); high_h(22)
            silu(23); high_h(23)

        @block.vector
        def _(dve):
            nc.vector.memset(decay[:, :, :], 0.0).then_inc(s_zero, 1)
            nc.vector.memset(ones[:, :], 1.0).then_inc(s_ones, 1)
            dve.wait_ge(s_vec, 16)
            nc.vector.tensor_scalar(tfc[:, :], vec[:, V_TF:V_TF + CC], F_MAX, None, ALU.min).then_inc(s_tfc, 1)
            dve.wait_ge(s_tfc, 1)
            nc.vector.tensor_scalar(nsc[:, :], tfc[:, :], 0.0, -1.0, ALU.max, ALU.mult).then_inc(s_tfc, 1)

            def decay_tile():
                dve.wait_ge(s_zero, 1)
                dve.wait_ge(s_dcol, 1)
                for c in range(CC):
                    cols = decay[:, c * UB:(c + 1) * UB, 2:PITCH]
                    last = nc.vector.tensor_scalar(cols, cols, dcol[:, c:c + 1], None, ALU.add)
                last.then_inc(s_decay, 1)

            def weights_any():
                dve.wait_ge(s_wsum, 2)
                nc.vector.tensor_scalar(wany[:, :], wsum[:, :], 0.0, None, ALU.is_gt).then_inc(s_wany, 1)

            def publish():
                dve.wait_ge(s_wcnt, 1)
                nc.vector.tensor_copy(flag[:, :], ps_d[0:1, 0, 0:1]).then_inc(s_flag, 1)

            def stats1(u):
                dve.wait_ge(s_xt[u], 16)
                if u >= 2:
                    dve.wait_ge(s_mv1, u - 1)
                for b in range(UB):
                    last = nc.vector.bn_stats(st1[:, u % 2, b, :], xt[:, u * UB + b, :])
                last.then_inc(s_st1, 1)

            def aggr1(u):
                dve.wait_ge(s_st1, u + 1)
                if u >= 2:
                    wait_turn(dve, s_kn, u - 2)
                for b in range(UB):
                    last = nc.vector.bn_aggr(mv1[:, u % 2, b, :], st1[:, u % 2, b, :])
                last.then_inc(s_mv1, 1)

            def eps1(u):
                dve.wait_ge(s_mv1, u + 1)
                if u >= 2:
                    dve.wait_ge(s_rs1, u - 1)
                nc.vector.tensor_scalar(ve1[:, u % 2, :], mv1[:, u % 2, :, 1], EPS, None, ALU.add).then_inc(s_ve1, 1)

            def pads(u):
                s = u % 2
                dve.wait_ge(s_ek, u + 1)
                nc.vector.tensor_copy(ek[:, s, :, 0:1], ek[:, s, :, 1:2]).then_inc(s_pad, 1)
                wait_turn(dve, s_pk, u)
                nc.vector.tensor_copy(pk[:, s, :, 0:1], pk[:, s, :, 1:2]).then_inc(s_pad, 1)

            def scan(u):
                s = u % 2
                if u == 0:
                    dve.wait_ge(s_decay, 1)
                if u >= 2:
                    dve.wait_ge(s_num, u - 1)
                dve.wait_ge(s_pad, 2 * u + 2)
                flat = [t.rearrange("p q t -> p (q t)") for t in (sbb[:, s, :, :], sa[:, s, :, :], decay[:, :, :],
                                                                  ek[:, s, :, :], pk[:, s, :, :])]
                nc.vector.tensor_tensor_scan(flat[0], flat[2], flat[3], 0.0, ALU.mult, ALU.add).then_inc(s_sb, 1)
                nc.vector.tensor_tensor_scan(flat[1], flat[2], flat[4], 0.0, ALU.mult, ALU.add).then_inc(s_sa, 1)

            def denom(u):
                s = u % 2
                if u == 0:
                    dve.wait_ge(s_f, 1)
                if u >= 2:
                    dve.wait_ge(s_ln, u - 1)
                dve.wait_ge(s_sb, u + 1)
                for c in range(CC):
                    q = slice(c * UB, (c + 1) * UB)
                    last = nc.vector.scalar_tensor_tensor(den[:, s, q, :], ek[:, s, q, 1:PITCH], fcol[:, c:c + 1],
                                                          sbb[:, s, q, 0:T], ALU.mult, ALU.add)
                last.then_inc(s_den, 1)

            def numer(u):
                s = u % 2
                if u >= 2:
                    wait_turn(dve, s_yk, u - 2)
                dve.wait_ge(s_sa, u + 1)
                for c in range(CC):
                    q = slice(c * UB, (c + 1) * UB)
                    last = nc.vector.scalar_tensor_tensor(num[:, s, q, :], pk[:, s, q, 1:PITCH], fcol[:, c:c + 1],
                                                          sa[:, s, q, 0:T], ALU.mult, ALU.add)
                last.then_inc(s_num, 1)

            def stats2(u):
                dve.wait_ge(s_x1T, u + 1)
                if u >= 1:
                    dve.wait_ge(s_mv2, u)
                for b in range(UB):
                    last = nc.vector.bn_stats(st2[:, b, :], ps_x[:, b * C:(b + 1) * C])
                last.then_inc(s_st2, 1)

            def aggr2(u):
                dve.wait_ge(s_st2, u + 1)
                if u >= 1:
                    dve.wait_ge(s_nb2, u)
                for b in range(UB):
                    last = nc.vector.bn_aggr(mv2[:, b, :], st2[:, b, :])
                last.then_inc(s_mv2, 1)

            def eps2(u):
                dve.wait_ge(s_mv2, u + 1)
                if u >= 1:
                    dve.wait_ge(s_rs2, u)
                nc.vector.tensor_scalar(ve2[:, :], mv2[:, :, 1], EPS, None, ALU.add).then_inc(s_ve2, 1)

            def bias2(u):
                dve.wait_ge(s_rs2, u + 1)
                if u >= 1:
                    dve.wait_ge(s_nt, u)
                nc.vector.scalar_tensor_tensor(nb2[:, :], mv2[:, :, 0], -1.0, rs2[:, :], ALU.mult,
                                               ALU.mult).then_inc(s_nb2, 1)

            def low_n(u):
                g = u // GU
                dve.wait_ge(s_xh, u + 1)
                if g >= 2:
                    dve.wait_ge(s_gu, MC * (g - 1))
                o = (u % GU) * UT
                nc.vector.tensor_tensor(xl[:, g % 2, :, o:o + UT], ps_x[:, :].rearrange("p (c n) -> p c n", c=CC),
                                        xh[:, g % 2, :, o:o + UT].bitcast(F32), ALU.subtract).then_inc(s_xl, 1)

            def gated(n):
                g, m = divmod(n, MC)
                dve.wait_ge(s_sil, n + 1)
                if n >= HS:
                    dve.wait_ge(s_hh, n - HS + 1)
                    wait_low(dve, n - HS)
                r = slice(0, P) if m < FULL else slice(REST, P)
                part = 1 if m < FULL else 0
                nc.vector.scalar_tensor_tensor(h[r, n % HS, :], ps_f[r, m % 2, part, :], vec[r, V_US + m:V_US + m + 1],
                                               sil[r, m % 2, :], ALU.mult, ALU.mult).then_inc(s_h, 1)

            def low_rest(n):
                dve.wait_ge(s_hh, n + 1)
                if n >= MC:
                    dve.wait_ge(s_dn, CC * (n - MC + 1))
                nc.vector.tensor_tensor(hx[0:REST, :], h[REST:P, n % HS, :], hx[REST:P, :].bitcast(F32),
                                        ALU.subtract).then_inc(s_hx, 1)

            def finish(g):
                wait_turn(dve, s_x1, GU * (g + 1) - 1)
                ts = slice(g * GT, (g + 1) * GT)
                for c in range(CC):
                    dve.wait_ge(s_dn, CC * (MC * (g + 1) - 1) + c + 1)
                    nc.vector.scalar_tensor_tensor(xc[:, c, ts], ps_d[:, c, :], vec[:, V_DS + c:V_DS + c + 1],
                                                   xc[:, c, ts], ALU.mult, ALU.add).then_inc(s_fin, 1)

            stats1(0); aggr1(0); eps1(0); stats1(1); aggr1(1); norm1(dve, 0); eps1(1); norm1(dve, 1)
            weigh(dve, 0); decay_tile(); pads(0); scan(0); weigh(dve, 1); denom(0); pads(1); numer(0); scan(1)
            stats1(2); divide(dve, 0); aggr1(2); add_y(dve, 0); eps1(2); stats1(3); denom(1); stats2(0)
            aggr1(3); aggr2(0); eps1(3); eps2(0); norm1(dve, 2); numer(1); stats1(4); bias2(0); norm1(dve, 3)
            divide(dve, 1); stats1(5); add_y(dve, 1); aggr1(4); pads(2); eps1(4); scan(2); low_n(0); denom(2)
            norm1(dve, 4); stats2(1); aggr1(5); aggr2(1); eps2(1); eps1(5); numer(2); pads(3); bias2(1)
            weights_any(); scan(3); stats1(6); publish(); denom(3); low_n(1); numer(3); stats2(2); norm1(dve, 5)
            aggr2(2); pads(4); eps2(2)
            gated(0); aggr1(6); eps1(6); bias2(2)
            gated(1); stats1(7); scan(4); denom(4); low_n(2); numer(4)
            gated(2); stats2(3); aggr1(7); aggr2(3); eps2(3); pads(5); norm1(dve, 6); bias2(3)
            gated(3); scan(5); eps1(7); denom(5)
            gated(4); low_n(3); stats2(4)
            gated(5); numer(5); norm1(dve, 7); pads(6); aggr2(4); eps2(4)
            gated(6); bias2(4); scan(6)
            gated(7); low_rest(5); denom(6); low_n(4); finish(0); stats2(5)
            gated(8); aggr2(5); eps2(5); numer(6); pads(7); bias2(5)
            gated(9); scan(7)
            gated(10); low_n(5); denom(7)
            gated(11); numer(7); stats2(6); aggr2(6); eps2(6); bias2(6)
            gated(12); low_rest(11); low_n(6)
            gated(13); stats2(7); aggr2(7); eps2(7)
            gated(14); bias2(7); finish(1)
            gated(15); low_n(7)
            gated(16)
            gated(17)
            gated(18); low_rest(17)
            gated(19)
            gated(20); finish(2)
            gated(21)
            gated(22)
            gated(23); low_rest(23); finish(3)

        @block.tensor
        def _(pe):
            HIGH, LOW = [(wgu_hi, wd_hi)], [(wgu_lo, wd_lo)]

            def k_T(u):
                wait_turn(pe, s_kn, u)
                if u == 0:
                    pe.wait_ge(s_ident, 1)
                else:
                    pe.wait_ge(s_ek, u)
                for b in range(UB):
                    for c in range(CC):
                        last = nc.tensor.transpose(ps_k[:, c, b, :], kn[:, u % 2, b, c * P:(c + 1) * P], ident[:, :])
                last.then_inc(s_kT, 1)

            def x1_T(u):
                wait_turn(pe, s_x1, u)
                if u >= 1:
                    pe.wait_ge(s_xl, u)
                for b in range(UB):
                    for c in range(CC):
                        t0 = u * UT + b * T
                        last = nc.tensor.transpose(ps_x[:, b * C + c * P:b * C + (c + 1) * P], xc[:, c, t0:t0 + T],
                                                   ident[:, :])
                last.then_inc(s_x1T, 1)

            def n_T(u):
                pe.wait_ge(s_nt, u + 1)
                for b in range(UB):
                    for c in range(CC):
                        last = nc.tensor.transpose(ps_x[:, c * UT + b * T:c * UT + (b + 1) * T],
                                                   nt[:, b, c * P:(c + 1) * P], ident[:, :])
                last.then_inc(s_nT, 1)

            def products(n, cols, weights):
                g, m = divmod(n, MC)
                for part, tile in (((0, m), (1, FULL + m)) if m < FULL else ((0, 2 * FULL),)):
                    todo = [(w, c, x) for w in weights for c in range(CC) for x in (xh, xl)]
                    for i, (w, c, x) in enumerate(todo):
                        last = nc.tensor.matmul(ps_f[:, m % 2, part, cols], w[0][:, c, tile, :], x[:, g % 2, c, cols],
                                                start=i == 0, stop=i == len(todo) - 1)
                return last

            def begin_gate_up(n):
                pe.wait_ge(s_whi, 1)
                pe.wait_ge(s_xl, 1)
                products(n, slice(0, UT), HIGH)

            def gate_up(n, weights):
                g, m = divmod(n, MC)
                if m == 0:
                    pe.wait_ge(s_xl, GU * (g + 1))
                if n >= 2:
                    pe.wait_ge(s_h, n - 1)
                begun = n < 2 and weights is HIGH
                products(n, slice(UT if begun else 0, GT), weights).then_inc(s_gu, 1)

            def down(n, weights):
                g, m = divmod(n, MC)
                if m == 0 and g >= 1:
                    pe.wait_ge(s_fin, CC * g)
                wait_low(pe, n)
                for c in range(CC):
                    todo = [(w, a) for w in weights for a in ((hh[:, m, :], hl[:, m, :]) if m < FULL else (hx[:, :],))]
                    for i, (w, a) in enumerate(todo):
                        last = nc.tensor.matmul(ps_d[:, c, :], w[1][:, m, c * P:(c + 1) * P], a,
                                                start=m == 0 and i == 0, stop=m == MC - 1 and i == len(todo) - 1)
                    last.then_inc(s_dn, 1)

            def count():
                pe.wait_ge(s_ones, 1)
                pe.wait_ge(s_wany, 1)
                nc.tensor.matmul(ps_d[0:1, 0, 0:1], ones[:, :], wany[:, 0:1], start=True, stop=False)
                nc.tensor.matmul(ps_d[0:1, 0, 0:1], ones[:, :], wany[:, 1:2], start=False, stop=True).then_inc(s_wcnt, 1)

            def feed_forward(weights):
                gate_up(0, weights)
                gate_up(1, weights); k_T(5)
                gate_up(2, weights); n_T(2); down(0, weights)
                gate_up(3, weights); x1_T(3); down(1, weights)
                gate_up(4, weights)
                gate_up(5, weights); n_T(3); down(2, weights); k_T(6); x1_T(4)
                gate_up(6, weights)
                gate_up(7, weights); down(3, weights)
                gate_up(8, weights); n_T(4); down(4, weights); k_T(7); down(5, weights); x1_T(5)
                gate_up(9, weights); down(6, weights)
                gate_up(10, weights); down(7, weights); n_T(5)
                gate_up(11, weights); down(8, weights); x1_T(6)
                gate_up(12, weights); down(9, weights)
                gate_up(13, weights); down(10, weights); n_T(6)
                gate_up(14, weights); x1_T(7); down(11, weights)
                gate_up(15, weights)
                gate_up(16, weights); n_T(7); down(12, weights)
                gate_up(17, weights); down(13, weights)
                gate_up(18, weights); down(14, weights)
                gate_up(19, weights); down(15, weights)
                gate_up(20, weights); down(16, weights)
                gate_up(21, weights); down(17, weights)
                gate_up(22, weights); down(18, weights)
                gate_up(23, weights); down(19, weights); down(20, weights); down(21, weights); down(22, weights)
                down(23, weights)

            k_T(0); k_T(1); x1_T(0); k_T(2); k_T(3); n_T(0); x1_T(1); k_T(4); begin_gate_up(0); begin_gate_up(1)
            count(); n_T(1); x1_T(2)
            pe.wait_ge(s_whi, 2)
            pe.wait_ge(s_wlo, len(PIECES))
            pe.wait_ge(s_flag, 1)
            found = pe.value_load(flag[0:1, 0:1], min_val=0, max_val=2 * P)
            with pe.If(found > 0):
                feed_forward(HIGH + LOW)
            with pe.Else():
                feed_forward(HIGH)
            pe.nop()


def kernel(x, ctx_2048, L0_xattn_time_decay, L0_xattn_time_first, L0_ffn_gate_w, L0_ffn_up_w, L0_ffn_down_w,
           L0_ffn_gate_s, L0_ffn_up_s, L0_ffn_down_s):
    import numpy as np
    import concourse.bacc as bacc
    from concourse.bass_utils import run_bass_kernel_spmd

    x, v = np.asarray(x), np.asarray(ctx_2048)
    cut = FULL * P

    def tiles(w, n):
        return w.reshape(n, P, -1).transpose(1, 0, 2)

    gT, uT = np.asarray(L0_ffn_gate_w).T, np.asarray(L0_ffn_up_w).T
    gu = np.concatenate([gT[:, :cut], uT[:, :cut], gT[:, cut:], uT[:, cut:]], axis=1)
    dT = np.asarray(L0_ffn_down_w).T
    dT = np.concatenate([dT[:cut], dT[cut:], dT[cut:]], axis=0)
    gs, us = np.asarray(L0_ffn_gate_s), np.asarray(L0_ffn_up_s)
    cols = [np.asarray(L0_xattn_time_decay), np.asarray(L0_xattn_time_first), np.concatenate([gs, gs[cut:]]),
            np.concatenate([us, us[cut:]]), np.asarray(L0_ffn_down_s)]
    arrays = {
        "x_tok": x,
        "x_ch": x.reshape(B * T, C).T,
        "v_ch": v.reshape(B * T, C).T,
        "w_gu": tiles(gu, CC).reshape(P, CC * GUC * P),
        "w_d": tiles(dT, MC).reshape(P, MC * C),
        "vecs": np.concatenate([a.reshape(-1, P) for a in cols], axis=0).T,
    }
    arrays = {k: np.ascontiguousarray(a) for k, a in arrays.items()}
    nc = bacc.Bacc("TRN2", target_bir_lowering=False, num_devices=1)
    args = [nc.dram_tensor(k, a.shape, F32, kind="ExternalInput").ap() for k, a in arrays.items()]
    out = nc.dram_tensor("out_ch", (C, B * T), F32, kind="ExternalOutput").ap()
    build(nc, *args, out)
    r = run_bass_kernel_spmd(nc, [arrays], core_ids=[0])
    return np.ascontiguousarray(r.results[0]["out_ch"].T).reshape(B, T, C)
```
